# Optimizing a Trainium2 kernel written in Bass

```python
import numpy as np
import jax
import jax.numpy as jnp

def _softmax(x, axis=-1):
    return jax.nn.softmax(x, axis=axis)

def _gelu(x):
    return jax.nn.gelu(x, approximate=True)

def _silu(x):
    return jax.nn.silu(x)

def _sigmoid(x):
    return jax.nn.sigmoid(x)

def _layernorm(x, axis=-1, eps=1e-05):
    m = jnp.mean(x, axis=axis, keepdims=True)
    v = jnp.var(x, axis=axis, keepdims=True)
    return (x - m) / jnp.sqrt(v + eps)

def _scatter_add(tgt, idx, src, axis=0):
    return tgt.at[idx].add(src)

def _segment_sum(src, seg, n):
    return jax.ops.segment_sum(src, seg, n)
kernel_name = 'mk_decoder_preln_d1_seqx_r8_570ccb'

def setup_inputs(seed: int=0):
    np.random.seed(seed)
    _w = jnp.asarray

    def _rec_inputs():
        import jax
        import jax.numpy as jnp
        _rk = jax.random.key(seed)
        x = -0.000125 + 0.9999 * jax.random.normal(jax.random.fold_in(_rk, 1), (4, 256, 256), jnp.float32)
        _lenS = 256 - jax.random.randint(jax.random.fold_in(_rk, 7), (4,), 0, max(1, 256 // 4) + 1, jnp.int32)
        _lenS2 = 256 - jax.random.randint(jax.random.fold_in(_rk, 8), (4,), 0, max(1, 256 // 4) + 1, jnp.int32)
        _ctx_2048P = jax.random.normal(jax.random.fold_in(_rk, 11), (4, 16, 256), jnp.float32)
        _ctx_2048c = jax.random.dirichlet(jax.random.fold_in(_rk, 511), 0.3 * jnp.ones((16,), jnp.float32), (4, 256))
        _ctx_2048t = jnp.einsum('bsk,bkd->bsd', _ctx_2048c, _ctx_2048P)
        _ctx_2048t = _ctx_2048t * jax.lax.rsqrt(jnp.mean(jnp.square(_ctx_2048t)) + 1e-12) * 0.953939
        ctx_2048 = -0.000514642 + 1.00011 * (_ctx_2048t + 0.3 * jax.random.normal(jax.random.fold_in(_rk, 611), (4, 256, 256), jnp.float32))
        _validS = jnp.arange(256)[None, :] < _lenS[:, None]
        _validS2 = jnp.arange(256)[None, :] < _lenS2[:, None]
        _causal = jnp.tril(jnp.ones((256, 256), dtype=bool))
        mask_BxS2_bk0 = jnp.logical_not(jnp.broadcast_to(_validS2[:, :], (4, 256)))
        return (x, ctx_2048, mask_BxS2_bk0)
    x, ctx_2048, mask_BxS2_bk0 = _rec_inputs()

    def _L0_attn_setup():
        import jax, jax.numpy as jnp
        import numpy as np
        import math
        EMBED_DIM = 256
        N_HEADS = 16
        HEAD_DIM = EMBED_DIM // N_HEADS
        THETA_BASE = 10000.0

        def _rope_freqs(seq_len):
            i = jnp.arange(HEAD_DIM // 2, dtype=jnp.float32)
            inv_freq = 1.0 / THETA_BASE ** (2.0 * i / HEAD_DIM)
            pos = jnp.arange(seq_len, dtype=jnp.float32)
            th = jnp.outer(pos, inv_freq)
            return (jnp.cos(th), jnp.sin(th))

        def _rope(t, cos, sin):
            b, h, s, d = t.shape
            tr = t.reshape(b, h, s, d // 2, 2)
            x0, x1 = (tr[..., 0], tr[..., 1])
            r0 = x0 * cos - x1 * sin
            r1 = x0 * sin + x1 * cos
            return jnp.stack([r0, r1], axis=-1).reshape(b, h, s, d)
        key = jax.random.key(seed)
        k1, k2, k3 = jax.random.split(key, 3)
        B, S = (2, 256)
        x = jax.random.normal(k1, (B, S, EMBED_DIM), jnp.float32)
        scale = EMBED_DIM ** (-0.5)
        Wqkv = jax.random.normal(k2, (EMBED_DIM, 3 * EMBED_DIM), jnp.float32) * scale
        Wo = jax.random.normal(k3, (EMBED_DIM, EMBED_DIM), jnp.float32) * scale
        return {'x': x, 'Wqkv': Wqkv, 'Wo': Wo}
    _L0_attn_all = _L0_attn_setup()
    _L0_attn_in = {k: v for k, v in _L0_attn_all.items() if k in ('Wqkv', 'Wo')}
    del _L0_attn_all

    def _L0_xattn_setup():
        import jax, jax.numpy as jnp
        import numpy as np
        key = jax.random.key(seed)
        k1, k2, k3 = jax.random.split(key, 3)
        B, S, D, M = (8, 256, 256, 128)
        hidden_states = jax.random.normal(k1, (B, S, D), dtype=jnp.float32)
        memory_tokens = jax.random.normal(k2, (B, M, D), dtype=jnp.float32)
        memory_mask = jax.random.randint(k3, (B, M), 0, 2).astype(jnp.bool_)
        return {'hidden_states': hidden_states, 'memory_tokens': memory_tokens, 'memory_mask': memory_mask}
    _L0_xattn_all = _L0_xattn_setup()
    _L0_xattn_in = {k: v for k, v in _L0_xattn_all.items() if k in ()}
    del _L0_xattn_all

    def _L0_ffn_setup():
        import jax, jax.numpy as jnp
        import numpy as np
        E = 8
        K = 2
        C = 256
        I = 176
        IS = I * 2
        B, T = (2, 256)
        key = jax.random.key(seed)
        ks = jax.random.split(key, 9)
        s = 0.02
        return {'x': jax.random.normal(ks[0], (B, T, C), dtype=jnp.float32), 'gate_w': jax.random.normal(ks[1], (E, C), dtype=jnp.float32) * s, 'w1': jax.random.normal(ks[2], (E, I, C), dtype=jnp.float32) * s, 'w2': jax.random.normal(ks[3], (E, I, C), dtype=jnp.float32) * s, 'w3': jax.random.normal(ks[4], (E, C, I), dtype=jnp.float32) * s, 'sw1': jax.random.normal(ks[5], (IS, C), dtype=jnp.float32) * s, 'sw2': jax.random.normal(ks[6], (IS, C), dtype=jnp.float32) * s, 'sw3': jax.random.normal(ks[7], (C, IS), dtype=jnp.float32) * s}
    _L0_ffn_all = _L0_ffn_setup()
    _L0_ffn_in = {k: v for k, v in _L0_ffn_all.items() if k in ('gate_w', 'w1', 'w2', 'w3', 'sw1', 'sw2', 'sw3')}
    del _L0_ffn_all
    return {'x': x, 'ctx_2048': ctx_2048, 'mask_BxS2_bk0': mask_BxS2_bk0, 'L0_attn_Wqkv': _L0_attn_in['Wqkv'], 'L0_attn_Wo': _L0_attn_in['Wo'], 'L0_ffn_gate_w': _L0_ffn_in['gate_w'], 'L0_ffn_w1': _L0_ffn_in['w1'], 'L0_ffn_w2': _L0_ffn_in['w2'], 'L0_ffn_w3': _L0_ffn_in['w3'], 'L0_ffn_sw1': _L0_ffn_in['sw1'], 'L0_ffn_sw2': _L0_ffn_in['sw2'], 'L0_ffn_sw3': _L0_ffn_in['sw3']}

def reference(x, ctx_2048, mask_BxS2_bk0, L0_attn_Wqkv, L0_attn_Wo, L0_ffn_gate_w, L0_ffn_w1, L0_ffn_w2, L0_ffn_w3, L0_ffn_sw1, L0_ffn_sw2, L0_ffn_sw3):
    import jax
    import jax.numpy as jnp

    def _L0_attn_ref(x, Wqkv, Wo):
        import jax, jax.numpy as jnp
        import numpy as np
        import math
        EMBED_DIM = 256
        N_HEADS = 16
        HEAD_DIM = EMBED_DIM // N_HEADS
        THETA_BASE = 10000.0

        def _rope_freqs(seq_len):
            i = jnp.arange(HEAD_DIM // 2, dtype=jnp.float32)
            inv_freq = 1.0 / THETA_BASE ** (2.0 * i / HEAD_DIM)
            pos = jnp.arange(seq_len, dtype=jnp.float32)
            th = jnp.outer(pos, inv_freq)
            return (jnp.cos(th), jnp.sin(th))

        def _rope(t, cos, sin):
            b, h, s, d = t.shape
            tr = t.reshape(b, h, s, d // 2, 2)
            x0, x1 = (tr[..., 0], tr[..., 1])
            r0 = x0 * cos - x1 * sin
            r1 = x0 * sin + x1 * cos
            return jnp.stack([r0, r1], axis=-1).reshape(b, h, s, d)
        B, S, E = x.shape
        H, D = (N_HEADS, E // N_HEADS)
        qkv = x @ Wqkv
        q, k, v = jnp.split(qkv, 3, axis=-1)
        heads = lambda t: t.reshape(B, S, H, D).transpose(0, 2, 1, 3)
        q, k, v = (heads(q), heads(k), heads(v))
        cos, sin = _rope_freqs(S)
        q = _rope(q, cos, sin)
        k = _rope(k, cos, sin)
        scores = jnp.einsum('bhqd,bhkd->bhqk', q, k) / math.sqrt(D)
        causal = jnp.tril(jnp.ones((S, S), dtype=bool))
        scores = jnp.where(causal, scores, -jnp.inf)
        attn = jax.nn.softmax(scores, axis=-1)
        op = jnp.einsum('bhqk,bhkd->bhqd', attn, v)
        op = op.transpose(0, 2, 1, 3).reshape(B, S, E)
        return op @ Wo

    def _L0_xattn_ref(hidden_states, memory_tokens, memory_mask):
        import jax, jax.numpy as jnp
        import numpy as np
        B, S, D = hidden_states.shape
        scale = 1.0 / jnp.sqrt(jnp.asarray(D, hidden_states.dtype))
        scores = jnp.einsum('bsd,bmd->bsm', hidden_states, memory_tokens) * scale
        neg_inf = jnp.asarray(-1e+30, scores.dtype)
        scores = jnp.where(memory_mask[:, None, :], scores, neg_inf)
        attn = jax.nn.softmax(scores, axis=-1)
        readout = jnp.einsum('bsm,bmd->bsd', attn, memory_tokens)
        valid_b = jnp.any(memory_mask, axis=-1)
        out = jnp.where(valid_b[:, None, None], readout, jnp.zeros_like(readout))
        return out

    def _L0_ffn_ref(x, gate_w, w1, w2, w3, sw1, sw2, sw3):
        import jax, jax.numpy as jnp
        import numpy as np
        E = 8
        K = 2
        C = 256
        I = 176
        IS = I * 2
        B, T = (2, 256)
        Bq, Tq, Cq = x.shape
        xf = x.reshape(-1, Cq)
        logits = xf @ gate_w.T
        probs = jax.nn.softmax(logits.astype(jnp.float32), axis=-1)
        topk_p, topk_i = jax.lax.top_k(probs, K)
        comb = (jax.nn.one_hot(topk_i, E, dtype=jnp.float32) * topk_p[..., None]).sum(axis=1).astype(x.dtype)
        h1 = jnp.einsum('nc,eic->eni', xf, w1)
        h2 = jnp.einsum('nc,eic->eni', xf, w2)
        h = jax.nn.silu(h1) * h2
        eo = jnp.einsum('eni,eci->enc', h, w3)
        y = jnp.einsum('enc,ne->nc', eo, comb).reshape(Bq, Tq, Cq)
        sh = jax.nn.silu(xf @ sw1.T) * (xf @ sw2.T) @ sw3.T
        return y + sh.reshape(Bq, Tq, Cq)
    x = x + _L0_attn_ref(_layernorm(x, axis=-1), L0_attn_Wqkv, L0_attn_Wo)
    x = x + _L0_xattn_ref(_layernorm(x, axis=-1), ctx_2048, mask_BxS2_bk0)
    x = x + _L0_ffn_ref(_layernorm(x, axis=-1), L0_ffn_gate_w, L0_ffn_w1, L0_ffn_w2, L0_ffn_w3, L0_ffn_sw1, L0_ffn_sw2, L0_ffn_sw3)
    return x

_drawn_inputs = setup_inputs


def setup_inputs(seed=0):
    import zlib

    import numpy as np

    out = dict(_drawn_inputs(seed))
    spreads = {}
    factors = {'L0_ffn_gate_w': 8.0,
     'L0_ffn_w1': 8.0,
     'L0_ffn_w2': 8.0,
     'L0_ffn_w3': 8.0,
     'L0_ffn_sw1': 3.526,
     'L0_ffn_sw2': 3.48,
     'L0_ffn_sw3': 3.506}
    for name, (base, spread) in spreads.items():
        noise = np.random.default_rng([zlib.crc32(name.encode()), seed]).standard_normal(out[name].shape)
        drawn = base * np.exp(spread * noise) if base else spread * noise
        out[name] = jnp.asarray(drawn.astype(out[name].dtype))
    for name, factor in factors.items():
        out[name] = (out[name] * factor).astype(out[name].dtype)
    return out
```

```python
from contextlib import ExitStack

import concourse.bass as bass
from concourse import mybir

ALU = mybir.AluOpType
ACT = mybir.ActivationFunctionType
AX = mybir.AxisListType
F32 = mybir.dt.float32
F32R = mybir.dt.float32r
BF16 = mybir.dt.bfloat16
FP16 = mybir.dt.float16
U8 = mybir.dt.uint8

P = 128
B, S, C = 4, 256, 256
NT = S // P
KC = C // P
H, DH = 16, 16
PAIRS = H // 2
SLOT = 64
KROWS = 3 * DH
G = 4
NG = H // G
VP = DH + 1
E, I, IS = 8, 176, 352
FT = 14
FE = E * I // P
GT = 512
EPS = 1e-5
NEG = -1e30


def decoder_layer(nc, x, ctx, ctx_t, mask, wqkv, wo, gate, w1, w2, w3, cos, sin, out):
    with ExitStack() as es:
        def sb(name, shape, dt=F32):
            return es.enter_context(nc.sbuf_tensor(name, shape, dt))

        attention = ExitStack()

        def sa(name, shape, dt=F32):
            return attention.enter_context(nc.sbuf_tensor(name, shape, dt))

        def sem(name):
            return es.enter_context(nc.semaphore(name))

        comb_dram = nc.dram_tensor("comb_dram", (E, B * S), F32, kind="Internal").ap()

        res = sb("res", [P, B * NT, C])
        gate_raw = sb("gate_raw", [P, KC, E])
        gate_hi = sb("gate_hi", [P, KC, E], F32R)
        gate_lo = sb("gate_lo", [P, KC, E], F32R)
        w_raw = sb("w_raw", [P, KC, FT * P])
        w1_hi = sb("w1_hi", [P, KC, FT * P], F32R)
        w1_lo = sb("w1_lo", [P, KC, FT * P], F32R)
        cos_t = sb("cos_t", [P, NT, DH // 2])
        sin_t = sb("sin_t", [P, NT, 2, DH // 2])
        mask_u8 = sb("mask_u8", [P, B, S], U8)
        mask_add = sb("mask_add", [P, B, S])
        valid = sb("valid", [P, B])
        ident = sb("ident", [P, P])
        ident_b = sb("ident_b", [P, P], BF16)
        causal_b = sb("causal_b", [P, P], BF16)
        earlier = sb("earlier", [P, E, E])
        epsb = sb("epsb", [P, 2])
        pw = sb("pw", [P, 2])
        stats = sb("stats", [P, 3, NT, 6])
        mv = sb("mv", [P, 3, NT, 2])
        vare = sb("vare", [P, 3, NT])
        rstd = sb("rstd", [P, 3, NT])
        x3_hi = sb("x3_hi", [P, KC, B * S], F32R)
        x3_lo = sb("x3_lo", [P, KC, B * S], F32R)
        xs_max = sb("xs_max", [P, NT])
        xs_neg = sb("xs_neg", [P, NT])
        xs_sum = sb("xs_sum", [P, NT])
        xs_rec = sb("xs_rec", [P, NT])
        xs_coef = sb("xs_coef", [P, NT])
        g_max = sb("g_max", [P, NT])
        g_sub = sb("g_sub", [P, NT, E])
        g_exp = sb("g_exp", [P, NT, E])
        g_sum = sb("g_sum", [P, NT])
        g_rec = sb("g_rec", [P, NT])
        g_p = sb("g_p", [P, NT, E])
        g_gt = sb("g_gt", [P, NT, E, E])
        g_eq = sb("g_eq", [P, NT, E, E])
        g_rank = sb("g_rank", [P, NT, E])
        comb = sb("comb", [P, NT, E])
        comb_t = sb("comb_t", [E, NT, P])

        wqkv_raw = sa("wqkv_raw", [P, KC, 3 * C])
        wqkv_hi = sa("wqkv_hi", [P, KC, 3 * C], F32R)
        wqkv_lo = sa("wqkv_lo", [P, KC, 3 * C], F32R)
        wo_raw = sa("wo_raw", [P, KC, C])
        wo_hi = sa("wo_hi", [P, KC, C], F32R)
        wo_lo = sa("wo_lo", [P, KC, C], F32R)
        xn = sa("xn", [P, 3, NT, C])
        xn_hi = [sa(f"xn{i}_hi", [P, KC, S], F32R) for i in range(2)]
        xn_lo = [sa(f"xn{i}_lo", [P, KC, S], F32R) for i in range(2)]
        rope_c = sa("rope_c", [P, 2, 2 * H, DH // 2])
        rope_s = sa("rope_s", [P, 2, 2 * H, DH // 2])
        rot = sa("rot", [P, 2 * H, DH])
        stk = sa("stk", [P, 2 * H, SLOT], F32R)
        q_t = sa("q_t", [P, 1, PAIRS, S], F32R)
        k_t = sa("k_t", [P, 1, PAIRS, S], F32R)
        negm = sa("negm", [P, NT, 2, PAIRS])
        negm_t = sa("negm_t", [H, NT, P], F32R)
        v_st = sa("v_st", [P, 2, NT, H, 3, VP], BF16)
        v_r1 = sa("v_r1", [P, NT, C])
        prob = sa("prob", [P, 2, 3, 512])
        prob_hi = sa("prob_hi", [P, 2, 3, 512], FP16)
        prob_lo = sa("prob_lo", [P, 2, 3, 512], FP16)
        o_sum = sa("o_sum", [P, NT, H, VP])
        o_rec = sa("o_rec", [P, NT, H, 1])
        o_n = sa("o_n", [P, NT, H, DH])
        o_hi = sa("o_hi", [P, KC, S], F32R)
        o_lo = sa("o_lo", [P, KC, S], F32R)
        ctx_raw = sa("ctx_raw", [P, 1, NT, C])
        ctx_hi = sa("ctx_hi", [P, NT, C], F32R)
        ctx_lo = sa("ctx_lo", [P, NT, C], F32R)
        ctxt_raw = sa("ctxt_raw", [P, 1, KC, S])
        ctxt_hi = sa("ctxt_hi", [P, KC, S], F32R)
        ctxt_lo = sa("ctxt_lo", [P, KC, S], F32R)
        xs = sa("xs", [P, NT, S])
        xp_hi = sa("xp_hi", [P, NT, S], F32R)
        xp_lo = sa("xp_lo", [P, NT, S], F32R)
        attention.close()
        w2_lo = sb("w2_lo", [P, KC, FT * P], F32R)
        w2_hi = sb("w2_hi", [P, KC, FT * P], F32R)
        w3_hi = sb("w3_hi", [P, FT, C], F32R)
        w3_lo = sb("w3_lo", [P, FT, C], F32R)
        comb_b = sb("comb_b", [P, FE, GT])
        h_s = sb("h_s", [P, 2, GT])
        h_c = sb("h_c", [P, 2, GT])
        h_hi = sb("h_hi", [P, 2, GT], F32R)
        h_lo = sb("h_lo", [P, 2, GT], F32R)

        bank = [es.enter_context(nc.psum_tensor(f"bank{i}", [P, 512], F32)) for i in range(8)]
        ps_x1, ps_qk, ps_tr, ps_out = bank[0], bank[1], bank[2], bank[7]
        ps_st = [bank[3], bank[4]]
        ps_s = [bank[5], bank[6]]

        names = """x_in0 x_in1 x_in2 x_in3 w_in wo_in gate_in ffn_in0 ffn_in1 ffn_in2 tab_in mask_in ctx_in0 ctx_in1 ctxt_in0 ctxt_in1
        const pool_chain dve_chain act_chain wqkv_ok wo_ok gate_ok w1_ok w2_ok w3_ok mask_ok
        ln_mv ln_rstd ln_xn xnt_ps xn_hi_ok xn_lo_ok qk_ps v_ps rope_ok rot_ok v_hi v_ok v_mid
        stk_hi stk_lo st_ps st_act st_dve sm_ps sm_max mt_ps mt_ok shift_ok
        s_ps p_exp p_masked p_hi p_lo o_ps o_ok on_ok ot_ps oh_ok ol_ok wo_ps x1_ok
        ctx_ok xs_ps xs_ok xp_ok xpt_ps xph_ok xpl_ok ro_ps x2_ok
        lg_ps g_ready g_exp_ok comb_ok ct_ps ct_ok ct_out cb_in h_ps1 h_ps2 hs_ok hg_ok hc_ok hhi_ok hlo_ok
        w3_done y_ps y_ok out_done""".split()
        s = {n: sem(n) for n in names}

        block = es.enter_context(nc.Block())

        def head(g, i):
            return 2 * (G * (g // 2) + i) + g % 2

        def halves(a_hi, a_lo, b_hi, b_lo):
            return ((a_hi, b_hi), (a_hi, b_lo), (a_lo, b_hi))

        @block.sync
        def _(sp):
            for b in range(B):
                sp.dma_start(res[:, b * NT:(b + 1) * NT, :],
                             x[b].rearrange("(t p) c -> p t c", p=P)).then_inc(s[f"x_in{b}"], 16)
                if b == 0:
                    sp.dma_start(wqkv_raw[:], wqkv.rearrange("(k p) n -> p k n", p=P)).then_inc(s["w_in"], 16)
                    sp.dma_start(cos_t[:], cos.rearrange("(t p) i -> p t i", p=P)).then_inc(s["tab_in"], 16)
                    sp.dma_start(sin_t[:], sin.rearrange("(t p) a i -> p t a i", p=P)).then_inc(s["tab_in"], 16)
            sp.dma_start(wo_raw[:], wo.rearrange("(k p) n -> p k n", p=P)).then_inc(s["wo_in"], 16)
            sp.dma_start(gate_raw[:], gate.rearrange("(k p) n -> p k n", p=P)).then_inc(s["gate_in"], 16)
            sp.dma_start(mask_u8[:], mask[None, :, :].broadcast_to([P, B, S])).then_inc(s["mask_in"], 16)
            sp.dma_start(w_raw[:], w1.rearrange("(k p) n -> p k n", p=P)).then_inc(s["ffn_in0"], 16)
            for b in range(B):
                if b:
                    sp.wait_ge(s["ctx_ok"], 4 * b)
                sp.dma_start(ctx_raw[:, 0], ctx[b].rearrange("(t p) c -> p t c", p=P)).then_inc(s[f"ctx_in{b % 2}"], 16)
                sp.dma_start(ctxt_raw[:, 0], ctx_t[b].rearrange("(k p) n -> p k n", p=P)).then_inc(s[f"ctxt_in{b % 2}"], 16)
                sp.wait_ge(s["mt_ok"], b + 1)
                for par in range(2):
                    sp.dma_start(q_t[SLOT * par + KROWS:SLOT * par + KROWS + 1, 0, :, :].bitcast(F32),
                                 negm_t[PAIRS * par:PAIRS * (par + 1), :, :].bitcast(F32)).then_inc(s["shift_ok"], 16)
                if b == 0:
                    sp.wait_ge(s["w1_ok"], 2)
                    sp.dma_start(w_raw[:], w2.rearrange("(k p) n -> p k n", p=P)).then_inc(s["ffn_in1"], 16)
                sp.wait_ge(s["ct_ok"], b + 1)
                sp.dma_start(comb_dram[:, b * S:(b + 1) * S], comb_t[:].rearrange("e t p -> e (t p)"))\
                    .then_inc(s["ct_out"], 16)
                if b == B - 1:
                    sp.wait_ge(s["w2_ok"], 2)
                    sp.dma_start(w_raw[:].rearrange("p k (f c) -> p (k f) c", c=C),
                                 w3.rearrange("(f p) c -> p f c", p=P)).then_inc(s["ffn_in2"], 16)
            sp.wait_ge(s["ct_out"], 16 * B)
            for g in range(2):
                if g:
                    sp.wait_ge(s["hc_ok"], FT)
                for e in range(E):
                    r = e * I
                    while r < (e + 1) * I:
                        j, p0 = divmod(r, P)
                        n = min(P - p0, (e + 1) * I - r)
                        sp.dma_start(comb_b[p0:p0 + n, j, :],
                                     comb_dram[e:e + 1, g * GT:(g + 1) * GT].broadcast_to([n, GT]))\
                            .then_inc(s["cb_in"], 16)
                        r += n
            for t in range(B * NT):
                sp.wait_ge(s["y_ok"], t + 1)
                sp.dma_start(out[t // NT, (t % NT) * P:(t % NT + 1) * P, :], res[:, t, :]).then_inc(s["out_done"], 16)
            sp.wait_ge(s["out_done"], 16 * B * NT)

        CB = sum(1 for e in range(E) for r in range(e * I, (e + 1) * I) if r == e * I or r % P == 0)

        @block.gpsimd
        def _(eng):
            chain = [0]

            def link(ins):
                chain[0] += 1
                ins.then_inc(s["pool_chain"], 1)
                eng.wait_ge(s["pool_chain"], chain[0])

            def split(src, hi, lo, ok):
                link(eng.tensor_scalar(hi, src, 1.0, None, ALU.mult))
                eng.tensor_tensor(lo, src, hi.bitcast(F32), ALU.subtract).then_inc(ok, 2)

            eng.memset(epsb[:], EPS)
            eng.memset(pw[:], -0.5)
            eng.memset(ident_b[:], 0.0)
            eng.memset(causal_b[:], 0.0)
            eng.memset(earlier[:], 1.0)
            link(eng.memset(ident[:], 0.0))
            eng.affine_select(out=ident[:], in_=ident[:], compare_op=ALU.not_equal, fill=1.0, base=0,
                              pattern=[[-1, P]], channel_multiplier=1)
            eng.affine_select(out=ident_b[:], in_=ident_b[:], compare_op=ALU.not_equal, fill=1.0, base=0,
                              pattern=[[-1, P]], channel_multiplier=1)
            eng.affine_select(out=causal_b[:], in_=causal_b[:], compare_op=ALU.is_ge, fill=NEG, base=0,
                              pattern=[[-1, P]], channel_multiplier=1)
            link(eng.affine_select(out=earlier[:], in_=earlier[:], compare_op=ALU.is_gt, fill=0.0, base=0,
                              pattern=[[1, E], [-1, E]], channel_multiplier=0))
            eng.memset(epsb[:], EPS).then_inc(s["const"], 1)

            def ln_rstd(n, i):
                eng.wait_ge(s["ln_mv"], i)
                link(eng.tensor_scalar(vare[:, n, :], mv[:, n, :, 1], EPS, None, ALU.add))
                eng.tensor_tensor(rstd[:, n, :], vare[:, n, :], pw[:], ALU.pow).then_inc(s["ln_rstd"], 1)

            for b in range(B):
                ln_rstd(0, 3 * b + 1)
                if b == 0:
                    eng.wait_ge(s["w_in"], 16)
                    split(wqkv_raw[:], wqkv_hi[:], wqkv_lo[:], s["wqkv_ok"])
                for t in range(NT):
                    n = NT * b + t
                    eng.wait_ge(s["rope_ok"], n + 1)
                    if n:
                        eng.wait_ge(s["stk_lo"], n)
                    eng.tensor_tensor(rot[:].rearrange("p g (a i) -> p a g i", a=2), rope_c[:], rope_s[:], ALU.add)\
                        .then_inc(s["rot_ok"], 1)
                if b == 0:
                    eng.wait_ge(s["wo_in"], 16)
                    split(wo_raw[:], wo_hi[:], wo_lo[:], s["wo_ok"])
                    eng.wait_ge(s["gate_in"], 16)
                    split(gate_raw[:], gate_hi[:], gate_lo[:], s["gate_ok"])
                    eng.wait_ge(s["mask_in"], 16)
                    eng.tensor_scalar(mask_add[:], mask_u8[:], -1.0, -NEG, ALU.add, ALU.mult).then_inc(s["mask_ok"], 1)
                for g in range(NG):
                    n = NG * b + g
                    for i in range(3):
                        eng.wait_ge(s["p_exp"], 3 * n + i + 1)
                        if i < 2:
                            v = prob[:, g % 2, i, :].rearrange("p (h q) -> p h q", h=2)[:, :, 0:P]
                        else:
                            v = prob[:, g % 2, i, :].rearrange("p (h q) -> p h q", h=G)
                        eng.affine_select(out=v, in_=v, compare_op=ALU.is_ge, fill=0.0, base=0,
                                          pattern=[[0, v.shape[1]], [1, P]], channel_multiplier=-1)\
                            .then_inc(s["p_masked"], 1)
                    eng.wait_ge(s["p_masked"], 3 * n + 3)
                    if n >= 2:
                        eng.wait_ge(s["o_ps"], n - 1)
                    eng.tensor_scalar(prob_hi[:, g % 2], prob[:, g % 2], 1.0, None, ALU.mult).then_inc(s["p_hi"], 1)
                    if g == 0:
                        if b:
                            eng.wait_ge(s["ro_ps"], NT * b)
                        eng.wait_ge(s[f"ctx_in{b % 2}"], 16 * (b // 2 + 1))
                        split(ctx_raw[:, 0], ctx_hi[:], ctx_lo[:], s["ctx_ok"])
                        eng.wait_ge(s[f"ctxt_in{b % 2}"], 16 * (b // 2 + 1))
                        split(ctxt_raw[:, 0], ctxt_hi[:], ctxt_lo[:], s["ctx_ok"])
                ln_rstd(1, 3 * b + 2)
                ln_rstd(2, 3 * b + 3)
                if b == 0:
                    eng.wait_ge(s["ffn_in0"], 16)
                    split(w_raw[:], w1_hi[:], w1_lo[:], s["w1_ok"])
            eng.wait_ge(s["ffn_in1"], 16)
            eng.wait_ge(s["ct_ok"], B)
            split(w_raw[:], w2_hi[:], w2_lo[:], s["w2_ok"])
            eng.wait_ge(s["ffn_in2"], 16)
            eng.wait_ge(s["ct_ok"], B)
            for n in range(FT):
                j = (n + FE) % FT
                split(w_raw[:].rearrange("p k (f c) -> p (k f) c", c=C)[:, j], w3_hi[:, j], w3_lo[:, j], s["w3_ok"])

        @block.scalar
        def _(act):
            def xn_hi_copy(n, i, dst):
                act.wait_ge(s["xnt_ps"], i)
                act.copy(dst, (ps_x1 if n == 0 else ps_tr)[:].rearrange("p (k t) -> p k t", k=KC))\
                    .then_inc(s["xn_hi_ok"], 1)

            for b in range(B):
                xn_hi_copy(0, 3 * b + 1, xn_hi[0][:])
                act.wait_ge(s["v_ps"], b + 1)
                act.copy(v_st[:, b % 2, :, :, 0, 0:DH], ps_x1[:].rearrange("p (t h d) -> p t h d", t=NT, d=DH))\
                    .then_inc(s["v_hi"], 1)
                for t in range(NT):
                    n = NT * b + t
                    act.wait_ge(s["rot_ok"], n + 1)
                    if n:
                        act.wait_ge(s["st_ps"], 4 * n)
                    act.copy(stk[:, :, 0:DH], rot[:])
                    act.copy(stk[:, 0:H, 2 * DH:3 * DH], rot[:, 0:H, :])
                    act.copy(stk[:, H:2 * H, DH:2 * DH], rot[:, H:2 * H, :]).then_inc(s["stk_hi"], 1)
                    if t == 0:
                        act.wait_ge(s["v_mid"], 2 * b + 1)
                        act.copy(v_st[:, b % 2, :, :, 1, 0:DH], v_r1[:].rearrange("p t (h d) -> p t h d", d=DH))\
                            .then_inc(s["v_hi"], 1)
                    for c in (0, 2):
                        act.wait_ge(s["st_ps"], 4 * n + c + 1)
                        dst = q_t if c < 2 else k_t
                        act.copy(dst[:, 0, 4 * (c % 2):4 * (c % 2) + 4, t * P:(t + 1) * P],
                                 ps_st[c % 2][:].rearrange("p (j q) -> p j q", j=4)).then_inc(s["st_act"], 1)
                act.wait_ge(s["mt_ps"], b + 1)
                if b:
                    act.wait_ge(s["shift_ok"], 32 * b)
                act.copy(negm_t[:], ps_st[0][0:H, 0:S].rearrange("h (t q) -> h t q", t=NT)).then_inc(s["mt_ok"], 1)
                for g in range(NG):
                    for i in range(3):
                        n = 3 * (NG * b + g) + i
                        act.wait_ge(s["s_ps"], n + 1)
                        if NG * b + g >= 2:
                            act.wait_ge(s["p_lo"], NG * b + g - 1)
                        act.activation(prob[:, g % 2, i, :], ps_s[n % 2][:], ACT.Exp, scale=DH ** -0.5)\
                            .then_inc(s["p_exp"], 1)
                act.wait_ge(s["ot_ps"], b + 1)
                act.copy(o_hi[:], ps_tr[:].rearrange("p (k t) -> p k t", k=KC)).then_inc(s["oh_ok"], 1)
                xn_hi_copy(1, 3 * b + 2, xn_hi[1][:])
                act.wait_ge(s["xs_ok"], b + 1)
                for t in range(NT):
                    act.activation(xs[:, t, :], xs[:, t, :], ACT.Exp, bias=xs_neg[:, t:t + 1],
                                   accum_out=xs_sum[:, t:t + 1]).then_inc(s["xp_ok"], 1)
                act.wait_ge(s["xpt_ps"], b + 1)
                act.copy(xp_hi[:], ps_tr[:].rearrange("p (k t) -> p k t", k=KC)).then_inc(s["xph_ok"], 1)
                xn_hi_copy(2, 3 * b + 3, x3_hi[:, :, b * S:(b + 1) * S])
                act.wait_ge(s["g_ready"], b + 1)
                act.activation(g_exp[:], g_sub[:], ACT.Exp).then_inc(s["g_exp_ok"], 1)
                act.wait_ge(s["ct_ps"], b + 1)
                if b:
                    act.wait_ge(s["ct_out"], 16 * b)
                act.copy(comb_t[:], ps_out[0:E, 0:S].rearrange("e (t q) -> e t q", t=NT)).then_inc(s["ct_ok"], 1)
            for g in range(2):
                for n in range(FT):
                    m = FT * g + n
                    act.wait_ge(s["h_ps1"], m + 1)
                    if m >= 2:
                        act.wait_ge(s["hg_ok"], m - 1)
                    act.activation(h_s[:, m % 2], bank[4 + 2 * (m % 2)][:], ACT.Silu).then_inc(s["hs_ok"], 1)
                    act.wait_ge(s["hc_ok"], m + 1)
                    if m >= 2:
                        act.wait_ge(s["w3_done"], m - 1)
                    act.copy(h_hi[:, m % 2], h_c[:, m % 2]).then_inc(s["hhi_ok"], 1)

        @block.vector
        def _(dve):
            chain = [0]

            def link(ins):
                chain[0] += 1
                ins.then_inc(s["dve_chain"], 1)
                dve.wait_ge(s["dve_chain"], chain[0])

            def layernorm(b, n, i):
                for t in range(NT):
                    ins = dve.bn_stats(stats[:, n, t, :], res[:, NT * b + t, :])
                link(ins)
                for t in range(NT):
                    ins = dve.bn_aggr(mv[:, n, t, :], stats[:, n, t, :])
                ins.then_inc(s["ln_mv"], 1)
                dve.wait_ge(s["ln_rstd"], i)
                if b:
                    dve.wait_ge(s["xnt_ps"], i - 3)
                for t in range(NT):
                    ins = dve.tensor_scalar(xn[:, n, t, :], res[:, NT * b + t, :], mv[:, n, t, 0:1],
                                            rstd[:, n, t:t + 1], ALU.subtract, ALU.mult)
                ins.then_inc(s["ln_xn"], 1)

            def xn_lo_sub(n, i, hi, dst):
                dve.wait_ge(s["xn_hi_ok"], i)
                dve.tensor_tensor(dst, (ps_x1 if n == 0 else ps_tr)[:].rearrange("p (k t) -> p k t", k=KC),
                                  hi.bitcast(F32), ALU.subtract).then_inc(s["xn_lo_ok"], 1)

            dve.memset(stk[:].bitcast(F32), 0.0)
            dve.memset(v_st[:], 0.0).then_inc(s["dve_chain"], 1)
            chain[0] += 1
            dve.wait_ge(s["dve_chain"], chain[0])
            dve.memset(v_st[:, :, :, :, 0, DH:VP], 1.0)
            link(dve.memset(stk[:, H:2 * H, KROWS:KROWS + 1].bitcast(F32), 1.0))

            for b in range(B):
                dve.wait_ge(s[f"x_in{b}"], 16)
                layernorm(b, 0, 3 * b + 1)
                xn_lo_sub(0, 3 * b + 1, xn_hi[0][:], xn_lo[0][:])
                dve.wait_ge(s["v_hi"], 2 * b + 1)
                dve.tensor_tensor(v_r1[:].rearrange("p t (h d) -> p t h d", d=DH),
                                  ps_x1[:].rearrange("p (t h d) -> p t h d", t=NT, d=DH),
                                  v_st[:, b % 2, :, :, 0, 0:DH], ALU.subtract).then_inc(s["v_mid"], 1)
                if b == 0:
                    dve.wait_ge(s["tab_in"], 32)
                for t in range(NT):
                    n = NT * b + t
                    dve.wait_ge(s["qk_ps"], n + 1)
                    if n:
                        dve.wait_ge(s["rot_ok"], n)
                    qk = ps_qk[:].rearrange("p (a g i) -> p a g i", a=2, i=DH // 2)
                    dve.tensor_tensor(rope_c[:].rearrange("p a g i -> p (a g) i"), qk.rearrange("p a g i -> p (a g) i"),
                                      cos_t[:, t, None, :].broadcast_to([P, 4 * H, DH // 2]), ALU.mult)
                    for a in range(2):
                        ins = dve.tensor_tensor(rope_s[:, a], qk[:, 1 - a],
                                                sin_t[:, t, a, None, :].broadcast_to([P, 2 * H, DH // 2]), ALU.mult)
                    ins.then_inc(s["rope_ok"], 1)
                    dve.wait_ge(s["stk_hi"], n + 1)
                    dve.tensor_tensor(stk[:, 0:H, DH:2 * DH], rot[:, 0:H, :], stk[:, 0:H, 0:DH].bitcast(F32), ALU.subtract)
                    dve.tensor_tensor(stk[:, H:2 * H, 2 * DH:3 * DH], rot[:, H:2 * H, :],
                                      stk[:, H:2 * H, 0:DH].bitcast(F32), ALU.subtract).then_inc(s["stk_lo"], 1)
                    if t == 0:
                        dve.wait_ge(s["v_hi"], 2 * b + 2)
                        dve.tensor_tensor(v_st[:, b % 2, :, :, 2, 0:DH], v_r1[:].rearrange("p t (h d) -> p t h d", d=DH),
                                          v_st[:, b % 2, :, :, 1, 0:DH], ALU.subtract).then_inc(s["v_mid"], 1)
                    for c in (1, 3):
                        dve.wait_ge(s["st_ps"], 4 * n + c + 1)
                        dst = q_t if c < 2 else k_t
                        dve.tensor_copy(dst[:, 0, 4 * (c % 2):4 * (c % 2) + 4, t * P:(t + 1) * P],
                                        ps_st[c % 2][:].rearrange("p (j q) -> p j q", j=4)).then_inc(s["st_dve"], 1)
                if b:
                    dve.wait_ge(s["mt_ps"], b)
                for f in range(12):
                    dve.wait_ge(s["sm_ps"], 12 * b + f + 1)
                    if f < 4:
                        j = 4 * (f // 2)
                        dve.tensor_reduce(negm[:, 0, f % 2, j:j + 4], ps_st[f % 2][:].rearrange("p (j k) -> p j k", k=P),
                                          AX.X, ALU.max, negate=True).then_inc(s["sm_max"], 1)
                    else:
                        j = 2 * ((f - 4) // 2)
                        dve.tensor_reduce(negm[:, 1, f % 2, j:j + 2], ps_st[f % 2][:].rearrange("p (j k) -> p j k", k=S),
                                          AX.X, ALU.max, negate=True).then_inc(s["sm_max"], 1)
                for g in range(NG):
                    n = NG * b + g
                    dve.wait_ge(s["p_hi"], n + 1)
                    if n >= 2:
                        dve.wait_ge(s["o_ps"], n - 1)
                    dve.tensor_tensor(prob_lo[:, g % 2], prob[:, g % 2], prob_hi[:, g % 2], ALU.subtract)\
                        .then_inc(s["p_lo"], 1)
                    dve.wait_ge(s["o_ps"], n + 1)
                    reduce_parts(dve, o_sum, ps_out, g, s)
                dve.wait_ge(s["o_ok"], NT * NG * (b + 1))
                link(dve.reciprocal(o_rec[:], o_sum[:, :, :, DH:VP]))
                if b:
                    dve.wait_ge(s["ot_ps"], b)
                dve.tensor_tensor(o_n[:], o_sum[:, :, :, 0:DH], o_rec[:].broadcast_to([P, NT, H, DH]), ALU.mult)\
                    .then_inc(s["on_ok"], 1)
                dve.wait_ge(s["oh_ok"], b + 1)
                dve.tensor_tensor(o_lo[:], ps_tr[:].rearrange("p (k t) -> p k t", k=KC), o_hi[:].bitcast(F32),
                                  ALU.subtract).then_inc(s["ol_ok"], 1)
                rb = res[:, NT * b:NT * (b + 1), :]
                dve.wait_ge(s["wo_ps"], NT * (b + 1))
                dve.tensor_tensor(rb, ps_out[:].rearrange("p (t c) -> p t c", t=NT), rb, ALU.add).then_inc(s["x1_ok"], 1)
                dve.wait_ge(s["x1_ok"], b + 1)
                layernorm(b, 1, 3 * b + 2)
                xn_lo_sub(1, 3 * b + 2, xn_hi[1][:], xn_lo[1][:])
                if b == 0:
                    dve.wait_ge(s["mask_in"], 16)
                    link(dve.tensor_reduce(valid[:], mask_u8[:], AX.X, ALU.max))
                    dve.wait_ge(s["mask_ok"], 1)
                dve.wait_ge(s["xs_ps"], NT * (b + 1))
                for t in range(NT):
                    ins = dve.tensor_tensor_reduce(xs[:, t, :], ps_out[:, t * S:(t + 1) * S], mask_add[:, b, :],
                                                   C ** -0.5, -3e38, ALU.add, ALU.max, xs_max[:, t:t + 1])
                link(ins)
                dve.tensor_scalar(xs_neg[:], xs_max[:], -1.0, None, ALU.mult).then_inc(s["xs_ok"], 1)
                dve.wait_ge(s["xp_ok"], NT * (b + 1))
                link(dve.reciprocal(xs_rec[:], xs_sum[:]))
                link(dve.tensor_scalar(xs_coef[:], xs_rec[:], valid[:, b:b + 1], None, ALU.mult))
                dve.wait_ge(s["xph_ok"], b + 1)
                dve.tensor_tensor(xp_lo[:], ps_tr[:].rearrange("p (k t) -> p k t", k=KC), xp_hi[:].bitcast(F32),
                                  ALU.subtract).then_inc(s["xpl_ok"], 1)
                dve.wait_ge(s["ro_ps"], NT * (b + 1))
                for t in range(NT):
                    r1 = res[:, NT * b + t, :]
                    dve.scalar_tensor_tensor(out=r1, in0=ps_out[:, t * C:(t + 1) * C], scalar=xs_coef[:, t:t + 1],
                                             in1=r1, op0=ALU.mult, op1=ALU.add).then_inc(s["x2_ok"], 1)
                dve.wait_ge(s["x2_ok"], NT * (b + 1))
                layernorm(b, 2, 3 * b + 3)
                xn_lo_sub(2, 3 * b + 3, x3_hi[:, :, b * S:(b + 1) * S], x3_lo[:, :, b * S:(b + 1) * S])
                dve.wait_ge(s["lg_ps"], NT * (b + 1))
                lg = ps_out[:, 0:NT * E].rearrange("p (t e) -> p t e", t=NT)
                link(dve.tensor_reduce(g_max[:], lg, AX.X, ALU.max))
                dve.tensor_tensor(g_sub[:], lg, g_max[:, :, None].broadcast_to([P, NT, E]), ALU.subtract)\
                    .then_inc(s["g_ready"], 1)
                dve.wait_ge(s["g_exp_ok"], b + 1)
                link(dve.tensor_reduce(g_sum[:], g_exp[:], AX.X, ALU.add))
                link(dve.reciprocal(g_rec[:], g_sum[:]))
                link(dve.tensor_tensor(g_p[:], g_exp[:], g_rec[:, :, None].broadcast_to([P, NT, E]), ALU.mult))
                for t in range(NT):
                    one = g_p[:, t, :, None].broadcast_to([P, E, E])
                    other = g_p[:, t, None, :].broadcast_to([P, E, E])
                    dve.tensor_tensor(g_gt[:, t], other, one, ALU.is_gt)
                    ins = dve.tensor_tensor(g_eq[:, t], other, one, ALU.is_equal)
                link(ins)
                for t in range(NT):
                    ins = dve.tensor_tensor(g_eq[:, t], g_eq[:, t], earlier[:], ALU.mult)
                link(ins)
                link(dve.tensor_tensor(g_gt[:], g_gt[:], g_eq[:], ALU.add))
                link(dve.tensor_reduce(g_rank[:], g_gt[:], AX.X, ALU.add))
                dve.scalar_tensor_tensor(out=comb[:], in0=g_rank[:], scalar=2.0, in1=g_p[:], op0=ALU.is_lt,
                                         op1=ALU.mult).then_inc(s["comb_ok"], 1)
            for g in range(2):
                for n in range(FT):
                    m = FT * g + n
                    j = (n + FE) % FT
                    dve.wait_ge(s["hs_ok"], m + 1)
                    dve.wait_ge(s["h_ps2"], m + 1)
                    if m >= 2:
                        dve.wait_ge(s["hlo_ok"], m - 1)
                        dve.wait_ge(s["hhi_ok"], m - 1)
                    if j >= FE:
                        dve.tensor_tensor(h_c[:, m % 2], bank[5 + 2 * (m % 2)][:], h_s[:, m % 2], ALU.mult)\
                            .then_inc(s["hg_ok"], 1)
                        dve.wait_ge(s["hg_ok"], m + 1)
                        dve.sem_inc(s["hc_ok"], 1)
                    else:
                        dve.tensor_tensor(h_c[:, m % 2], bank[5 + 2 * (m % 2)][:], h_s[:, m % 2], ALU.mult)\
                            .then_inc(s["hg_ok"], 1)
                        dve.wait_ge(s["cb_in"], 16 * CB * (g + 1))
                        dve.wait_ge(s["hg_ok"], m + 1)
                        dve.tensor_tensor(h_c[:, m % 2], h_c[:, m % 2], comb_b[:, j, :], ALU.mult)\
                            .then_inc(s["hc_ok"], 1)
                    dve.wait_ge(s["hhi_ok"], m + 1)
                    dve.tensor_tensor(h_lo[:, m % 2], h_c[:, m % 2], h_hi[:, m % 2].bitcast(F32), ALU.subtract)\
                        .then_inc(s["hlo_ok"], 1)
                for t in range(4):
                    dve.wait_ge(s["y_ps"], 4 * g + t + 1)
                    dve.tensor_tensor(res[:, 4 * g + t, :], bank[t][:, 0:C], res[:, 4 * g + t, :], ALU.add)\
                        .then_inc(s["y_ok"], 1)

        @block.tensor
        def _(pe):
            def split_product(dst, lhs_hi, lhs_lo, rhs_hi, rhs_lo, kt=KC):
                for k in range(kt):
                    for i, (a, c) in enumerate(halves(lhs_hi, lhs_lo, rhs_hi, rhs_lo)):
                        ins = pe.matmul(dst, a(k), c(k), start=(k == 0 and i == 0), stop=(k == kt - 1 and i == 2))
                return ins

            def transposes(dst, src):
                for k in range(2):
                    for t in range(NT):
                        ins = pe.transpose(dst[:, k * S + t * P:k * S + (t + 1) * P], src(t, k), ident[:])
                return ins

            def head_rows(tensor, b, h, rows):
                r = SLOT * (h % 2)
                return tensor[r:r + rows, 0, h // 2, :]

            pe.wait_ge(s["const"], 1)
            for b in range(B):
                pe.wait_ge(s["ln_xn"], 3 * b + 1)
                if b:
                    pe.wait_ge(s["v_mid"], 2 * b - 1)
                transposes(ps_x1, lambda t, k: xn[:, 0, t, k * P:(k + 1) * P]).then_inc(s["xnt_ps"], 1)
                pe.wait_ge(s["xn_lo_ok"], 3 * b + 1)
                pe.wait_ge(s["wqkv_ok"], 2)
                for t in range(NT):
                    tok = slice(t * P, (t + 1) * P)
                    ins = split_product(ps_x1[:, t * C:(t + 1) * C], lambda k: xn_hi[0][:, k, tok],
                                        lambda k: xn_lo[0][:, k, tok],
                                        lambda k: wqkv_hi[:, k, 2 * C:3 * C], lambda k: wqkv_lo[:, k, 2 * C:3 * C])
                ins.then_inc(s["v_ps"], 1)
                for t in range(NT):
                    tok = slice(t * P, (t + 1) * P)
                    if NT * b + t:
                        pe.wait_ge(s["rope_ok"], NT * b + t)
                    split_product(ps_qk[:], lambda k: xn_hi[0][:, k, tok], lambda k: xn_lo[0][:, k, tok],
                                  lambda k: wqkv_hi[:, k, 0:2 * C], lambda k: wqkv_lo[:, k, 0:2 * C])\
                        .then_inc(s["qk_ps"], 1)
                for t in range(NT):
                    n = NT * b + t
                    pe.wait_ge(s["stk_lo"], n + 1)
                    for c in range(4):
                        if c % 2 == 0:
                            if 2 * n + c // 2:
                                pe.wait_ge(s["st_act"], 2 * n + c // 2)
                            if b and n % NT == 0 and c == 0:
                                pe.wait_ge(s["mt_ok"], b)
                        else:
                            if 2 * n + c // 2:
                                pe.wait_ge(s["st_dve"], 2 * n + c // 2)
                            if b and n % NT == 0 and c == 1:
                                pe.wait_ge(s["sm_max"], 12 * b)
                        for j in range(4):
                            h = 8 * c + 2 * j
                            ins = pe.transpose(ps_st[c % 2][:, j * P:(j + 1) * P],
                                               stk[:, h:h + 2, :].bitcast(F32).rearrange("p h r -> p (h r)"), ident[:])
                        ins.then_inc(s["st_ps"], 1)
                pe.wait_ge(s["st_act"], 2 * NT * (b + 1))
                pe.wait_ge(s["st_dve"], 2 * NT * (b + 1))
                for f in range(12):
                    if f >= 2:
                        pe.wait_ge(s["sm_max"], 12 * b + f - 1)
                    t = 0 if f < 4 else 1
                    keys = P * (t + 1)
                    for i in range(512 // keys):
                        h = 2 * (4 * (f // 2) + i if t == 0 else 2 * ((f - 4) // 2) + i) + f % 2
                        dst = ps_st[f % 2][:, i * keys:(i + 1) * keys]
                        pe.matmul(dst, head_rows(q_t, b, h, KROWS)[:, t * P:(t + 1) * P],
                                  head_rows(k_t, b, h, KROWS)[:, 0:keys], start=True, stop=True)
                        ins = pe.matmul(dst[:, t * P:keys], ident_b[:], causal_b[:], start=False, stop=True,
                                        skip_group_check=True)
                    ins.then_inc(s["sm_ps"], 1)
                pe.wait_ge(s["sm_max"], 12 * (b + 1))
                for t in range(NT):
                    ins = pe.transpose(ps_st[0][0:H, t * P:(t + 1) * P], negm[:, t].rearrange("p r j -> p (r j)"), ident[:])
                ins.then_inc(s["mt_ps"], 1)
                pe.wait_ge(s["shift_ok"], 32 * (b + 1))

                def scores(g):
                    for i in range(3):
                        n = 3 * (NG * b + g) + i
                        if n >= 2:
                            pe.wait_ge(s["p_exp"], n - 1)
                        heads = [head(g, 2 * i), head(g, 2 * i + 1)] if i < 2 else [head(g, j) for j in range(G)]
                        w = S if i < 2 else P
                        for c, h in enumerate(heads):
                            q0 = 0 if i < 2 else P
                            k0 = 0 if i < 2 else P
                            ins = pe.matmul(ps_s[n % 2][:, c * w:(c + 1) * w], head_rows(k_t, b, h, KROWS + 1)[:, k0:k0 + P],
                                            head_rows(q_t, b, h, KROWS + 1)[:, q0:S], start=True, stop=True)
                        ins.then_inc(s["s_ps"], 1)

                def values(g):
                    n = NG * b + g
                    pe.wait_ge(s["p_hi"], n + 1)
                    pe.wait_ge(s["p_lo"], n + 1)
                    if g == 0:
                        pe.wait_ge(s["v_mid"], 2 * (b + 1))
                    if n:
                        pe.wait_ge(s["o_ok"], NT * n)
                    if g == 0 and b:
                        pe.wait_ge(s["ct_ok"], b)
                    for t in range(NT):
                        for i in range(G):
                            o = (t * G + i) * 3 * VP
                            dst = ps_out[:, o:o + 3 * VP]
                            parts = [(pr, 0, i // 2, (i % 2) * S + t * P) for pr in (prob_hi, prob_lo)]
                            if t:
                                parts += [(pr, 1, 2, i * P) for pr in (prob_hi, prob_lo)]
                            for m, (pr, kt, blk, q0) in enumerate(parts):
                                ins = pe.matmul(dst, pr[:, g % 2, blk, q0:q0 + P],
                                                v_st[:, b % 2, kt, head(g, i)].rearrange("p a d -> p (a d)"),
                                                start=(m == 0), stop=(m == len(parts) - 1))
                    ins.then_inc(s["o_ps"], 1)

                scores(0)
                for g in range(NG):
                    if g + 1 < NG:
                        scores(g + 1)
                    values(g)
                pe.wait_ge(s["on_ok"], b + 1)
                if b:
                    pe.wait_ge(s["xn_lo_ok"], 3 * b)
                transposes(ps_tr, lambda t, k: o_n[:, t, k * 8:(k + 1) * 8, :].rearrange("p h d -> p (h d)"))\
                    .then_inc(s["ot_ps"], 1)
                pe.wait_ge(s["ol_ok"], b + 1)
                pe.wait_ge(s["wo_ok"], 2)
                pe.wait_ge(s["o_ok"], NT * NG * (b + 1))
                for t in range(NT):
                    tok = slice(t * P, (t + 1) * P)
                    split_product(ps_out[:, t * C:(t + 1) * C], lambda k: o_hi[:, k, tok], lambda k: o_lo[:, k, tok],
                                  lambda k: wo_hi[:, k, :], lambda k: wo_lo[:, k, :]).then_inc(s["wo_ps"], 1)
                pe.wait_ge(s["ln_xn"], 3 * b + 2)
                transposes(ps_tr, lambda t, k: xn[:, 1, t, k * P:(k + 1) * P]).then_inc(s["xnt_ps"], 1)
                pe.wait_ge(s["xn_lo_ok"], 3 * b + 2)
                pe.wait_ge(s["ctx_ok"], 4 * (b + 1))
                for t in range(NT):
                    tok = slice(t * P, (t + 1) * P)
                    split_product(ps_out[:, t * S:(t + 1) * S], lambda k: xn_hi[1][:, k, tok], lambda k: xn_lo[1][:, k, tok],
                                  lambda k: ctxt_hi[:, k, :], lambda k: ctxt_lo[:, k, :]).then_inc(s["xs_ps"], 1)
                pe.wait_ge(s["xp_ok"], NT * (b + 1))
                transposes(ps_tr, lambda t, k: xs[:, t, k * P:(k + 1) * P]).then_inc(s["xpt_ps"], 1)
                pe.wait_ge(s["xpl_ok"], b + 1)
                for t in range(NT):
                    tok = slice(t * P, (t + 1) * P)
                    split_product(ps_out[:, t * C:(t + 1) * C], lambda k: xp_hi[:, k, tok], lambda k: xp_lo[:, k, tok],
                                  lambda k: ctx_hi[:, k, :], lambda k: ctx_lo[:, k, :]).then_inc(s["ro_ps"], 1)
                pe.wait_ge(s["ln_xn"], 3 * b + 3)
                transposes(ps_tr, lambda t, k: xn[:, 2, t, k * P:(k + 1) * P]).then_inc(s["xnt_ps"], 1)
                pe.wait_ge(s["xn_lo_ok"], 3 * b + 3)
                pe.wait_ge(s["gate_ok"], 2)
                for t in range(NT):
                    tok = slice((NT * b + t) * P, (NT * b + t + 1) * P)
                    split_product(ps_out[:, t * E:(t + 1) * E], lambda k: x3_hi[:, k, tok], lambda k: x3_lo[:, k, tok],
                                  lambda k: gate_hi[:, k, :], lambda k: gate_lo[:, k, :]).then_inc(s["lg_ps"], 1)
                pe.wait_ge(s["comb_ok"], b + 1)
                for t in range(NT):
                    ins = pe.transpose(ps_out[0:E, t * P:(t + 1) * P], comb[:, t, :], ident[:])
                ins.then_inc(s["ct_ps"], 1)
            pe.wait_ge(s["w1_ok"], 2)
            pe.wait_ge(s["w2_ok"], 2)
            pe.wait_ge(s["ct_ok"], B)
            pe.wait_ge(s["xn_lo_ok"], 3 * B)

            def down(m):
                g, n = divmod(m, FT)
                j = (n + FE) % FT
                pe.wait_ge(s["hlo_ok"], m + 1)
                pe.wait_ge(s["hhi_ok"], m + 1)
                if not g:
                    pe.wait_ge(s["w3_ok"], 2 * (n + 1))
                for t in range(4):
                    if g and n == 0:
                        pe.wait_ge(s["y_ok"], t + 1)
                    tok = slice(t * P, (t + 1) * P)
                    for i, (a, c) in enumerate(halves(h_hi, h_lo, w3_hi, w3_lo)):
                        ins = pe.matmul(bank[t][:, 0:C], a[:, m % 2, tok], c[:, j, :],
                                        start=(n == 0 and i == 0), stop=(n == FT - 1 and i == 2))
                    if n == FT - 1:
                        ins.then_inc(s["y_ps"], 1)
                if n < FT - 1:
                    ins.then_inc(s["w3_done"], 1)
                else:
                    pe.wait_ge(s["y_ps"], 4 * (g + 1))
                    pe.sem_inc(s["w3_done"], 1)

            for m in range(2 * FT):
                g, n = divmod(m, FT)
                j = (n + FE) % FT
                if m >= 2:
                    pe.wait_ge(s["hg_ok"], m - 1)
                hid = slice(j * P, (j + 1) * P)
                tok = slice(g * GT, (g + 1) * GT)
                for w_hi, w_lo, bk, name in ((w1_hi, w1_lo, 4, "h_ps1"), (w2_hi, w2_lo, 5, "h_ps2")):
                    split_product(bank[bk + 2 * (m % 2)][:], lambda k: w_hi[:, k, hid], lambda k: w_lo[:, k, hid],
                                  lambda k: x3_hi[:, k, tok], lambda k: x3_lo[:, k, tok]).then_inc(s[name], 1)
                if m:
                    down(m - 1)
            down(2 * FT - 1)


def reduce_parts(dve, o_sum, ps_out, g, s):
    for t in range(NT):
        w = G * 3 * VP
        dve.tensor_reduce(o_sum[:, t].rearrange("p (j r) d -> p j r d", r=2)[:, G * (g // 2):G * (g // 2) + G, g % 2, :],
                          ps_out[:, t * w:(t + 1) * w].rearrange("p (h a d) -> p h d a", h=G, a=3), AX.X, ALU.add)\
            .then_inc(s["o_ok"], 1)


def kernel(**inputs):
    import numpy as np
    import concourse.bacc as bacc
    from concourse.bass_utils import run_bass_kernel_spmd

    a = {k: np.asarray(v) for k, v in inputs.items()}
    order = np.arange(C).reshape(H, DH // 2, 2).transpose(2, 0, 1).reshape(2, -1)
    columns = np.concatenate([order[0], C + order[0], order[1], C + order[1], 2 * C + np.arange(C)])
    hidden = FT * P

    def up(w, shared):
        return np.concatenate([w.reshape(E * I, C), shared, np.zeros((hidden - E * I - IS, C), w.dtype)]).T

    w3 = a["L0_ffn_w3"]
    down = np.concatenate([w3.transpose(0, 2, 1).reshape(E * I, C), a["L0_ffn_sw3"].T,
                           np.zeros((hidden - E * I - IS, C), w3.dtype)])
    inv = (1.0 / np.float32(10000.0) ** (2.0 * np.arange(DH // 2, dtype=np.float32) / DH)).astype(np.float32)
    angle = np.outer(np.arange(S, dtype=np.float32), inv).astype(np.float32)
    arrays = {
        "x": a["x"], "ctx": a["ctx_2048"], "ctx_t": a["ctx_2048"].transpose(0, 2, 1), "mask": a["mask_BxS2_bk0"],
        "wqkv": a["L0_attn_Wqkv"][:, columns], "wo": a["L0_attn_Wo"], "gate": a["L0_ffn_gate_w"].T,
        "w1": up(a["L0_ffn_w1"], a["L0_ffn_sw1"]), "w2": up(a["L0_ffn_w2"], a["L0_ffn_sw2"]), "w3": down,
        "cos": np.cos(angle), "sin": np.stack([-np.sin(angle), np.sin(angle)], axis=1),
    }
    arrays = {k: np.ascontiguousarray(v) for k, v in arrays.items()}
    nc = bacc.Bacc("TRN2", target_bir_lowering=False, num_devices=1)
    args = [nc.dram_tensor(k, v.shape, mybir.dt.from_np(v.dtype), kind="ExternalInput").ap() for k, v in arrays.items()]
    out = nc.dram_tensor("out", (B, S, C), F32, kind="ExternalOutput").ap()
    decoder_layer(nc, *args, out)
    r = run_bass_kernel_spmd(nc, [arrays], core_ids=[0])
    return r.results[0]["out"]
```

```python
from contextlib import ExitStack

import concourse.bass as bass
from concourse import mybir

ALU = mybir.AluOpType
ACT = mybir.ActivationFunctionType
AX = mybir.AxisListType
F32 = mybir.dt.float32
F32R = mybir.dt.float32r
BF16 = mybir.dt.bfloat16
FP16 = mybir.dt.float16
U8 = mybir.dt.uint8

P = 128
B, S, C = 4, 256, 256
NT = S // P
KC = C // P
H, DH = 16, 16
PAIRS = H // 2
SLOT = 64
KROWS = 3 * DH
G = 4
NG = H // G
VP = DH + 1
E, I, IS = 8, 176, 352
FT = 14
FE = E * I // P
GT = 512
EPS = 1e-5
NEG = -1e30


def decoder_layer(nc, x, ctx, ctx_t, mask, wqkv, wo, gate, w1, w2, w3, cos, sin, out):
    with ExitStack() as es:
        def sb(name, shape, dt=F32):
            return es.enter_context(nc.sbuf_tensor(name, shape, dt))

        def raw_and_lo(alloc, name, shape):
            with nc.sbuf_tensor(name + "_raw", shape, F32) as raw:
                pass
            return raw, alloc(name + "_lo", shape, F32R)

        attention = ExitStack()

        def sa(name, shape, dt=F32):
            return attention.enter_context(nc.sbuf_tensor(name, shape, dt))

        def sem(name):
            return es.enter_context(nc.semaphore(name))

        comb_dram = nc.dram_tensor("comb_dram", (E, B * S), F32, kind="Internal").ap()

        res = sb("res", [P, B * NT, C])
        gate_raw, gate_lo = raw_and_lo(sb, "gate", [P, KC, E])
        gate_hi = sb("gate_hi", [P, KC, E], F32R)
        w1_raw, w1_lo = raw_and_lo(sb, "w1", [P, KC, FT * P])
        w2_raw, w2_lo = raw_and_lo(sb, "w2", [P, KC, FT * P])
        w2_hi = sb("w2_hi", [P, KC, FT * P], F32R)
        w1_hi = sb("w1_hi", [P, KC, FT * P], F32R)
        cos_t = sb("cos_t", [P, NT, DH // 2])
        sin_t = sb("sin_t", [P, NT, 2, DH // 2])
        mask_u8 = sb("mask_u8", [P, B, S], U8)
        mask_add = sb("mask_add", [P, B, S], BF16)
        valid = sb("valid", [P, B])
        ident = sb("ident", [P, P])
        ident_b = sb("ident_b", [P, P], BF16)
        causal_b = sb("causal_b", [P, P], BF16)
        earlier = sb("earlier", [P, E, E])
        pw = sb("pw", [P, 2])
        stats = sb("stats", [P, 3, NT, 6])
        mv = sb("mv", [P, 3, NT, 2])
        vare = sb("vare", [P, 3, NT])
        rstd = sb("rstd", [P, 3, NT])
        x3_hi = sb("x3_hi", [P, KC, B * S], F32R)
        x3_lo = sb("x3_lo", [P, KC, B * S], F32R)
        xs_max = sb("xs_max", [P, NT])
        xs_neg = sb("xs_neg", [P, NT])
        xs_sum = sb("xs_sum", [P, NT])
        xs_rec = sb("xs_rec", [P, NT])
        xs_coef = sb("xs_coef", [P, NT])
        g_max = sb("g_max", [P, NT])
        g_sub = sb("g_sub", [P, NT, E])
        g_exp = sb("g_exp", [P, NT, E])
        g_sum = sb("g_sum", [P, NT])
        g_rec = sb("g_rec", [P, NT])
        g_p = sb("g_p", [P, NT, E])
        g_gt = sb("g_gt", [P, NT, E, E])
        g_eq = sb("g_eq", [P, NT, E, E])
        g_rank = sb("g_rank", [P, NT, E])
        comb = sb("comb", [P, NT, E])
        comb_t = sb("comb_t", [E, NT, P])

        o_sum = sb("o_sum", [P, NT, H, VP])
        o_rec = sb("o_rec", [P, NT, H, 1])
        tail = sb("tail", [P, NT, C])
        tail_hi = sb("tail_hi", [P, KC, S], F32R)
        tail_lo = sb("tail_lo", [P, KC, S], F32R)
        wo_raw, wo_lo = raw_and_lo(sb, "wo", [P, KC, C])
        wo_hi = sb("wo_hi", [P, KC, C], F32R)
        ctx_raw, ctx_lo = raw_and_lo(sb, "ctx", [P, NT, C])
        ctx_hi = sb("ctx_hi", [P, NT, C], F32R)
        ctxt_raw, ctxt_lo = raw_and_lo(sb, "ctxt", [P, KC, S])
        ctxt_hi = sb("ctxt_hi", [P, KC, S], F32R)
        wqkv_raw, wqkv_lo = raw_and_lo(sa, "wqkv", [P, KC, 3 * C])
        wqkv_hi = sa("wqkv_hi", [P, KC, 3 * C], F32R)
        xn1 = sa("xn1", [P, NT, C])
        xt_hi = sa("xt_hi", [P, KC, S], F32R)
        xt_lo = sa("xt_lo", [P, KC, S], F32R)
        rope_c = sa("rope_c", [P, 2, 2 * H, DH // 2])
        rope_s = sa("rope_s", [P, 2, 2 * H, DH // 2])
        rot = sa("rot", [P, 2, 2 * H, DH])
        stk = sa("stk", [P, 2 * H, SLOT], F32R)
        q_t = sa("q_t", [P, 2, PAIRS, S], F32R)
        k_t = sa("k_t", [P, 2, PAIRS, S], F32R)
        v_r1 = sa("v_r1", [P, NT, C])
        negm = sa("negm", [P, NT, 2, PAIRS])
        negm_t = sa("negm_t", [H, NT, P], F32R)
        v_st = sa("v_st", [P, 2, NT, H, 3, VP], BF16)
        prob = sa("prob", [P, 2, 3, 512])
        prob_hi = sa("prob_hi", [P, 2, 3, 512], FP16)
        prob_lo = sa("prob_lo", [P, 2, 3, 512], FP16)
        attention.close()
        w3_raw, w3_lo = raw_and_lo(sb, "w3", [P, FT, C])
        w3_hi = sb("w3_hi", [P, FT, C], F32R)
        h_s = sb("h_s", [P, 2, GT])
        h_c = sb("h_c", [P, 2, GT])
        h_hi = sb("h_hi", [P, 2, GT], F32R)
        h_lo = sb("h_lo", [P, 2, GT], F32R)
        comb_b = sb("comb_b", [P, FE, GT])

        bank = [es.enter_context(nc.psum_tensor(f"bank{i}", [P, 512], F32)) for i in range(8)]
        ps_x1, ps_qk, ps_tail, ps_out = bank[0], bank[1], bank[2], bank[7]
        ps_st = [bank[3], bank[4]]
        ps_s = [bank[5], bank[6]]
        h1_bank, h2_bank = [bank[3], bank[4]], [bank[5], bank[6]]

        def y_tile(t):
            return bank[t // 2][:, t % 2 * C:(t % 2 + 1) * C]

        names = """x_in0 x_in1 x_in2 x_in3 w_in wo_in gate_in w1_in w2_in w3_in tab_in mask_in ctx_in ctxt_in
        const pool_chain dve_chain wqkv_hi_ok wqkv_ok wo_ok gate_ok w1_ok w2_ok w3_ok mask_ok
        qk_ps v_ps rope_ok rot_ok v_hi v_mid
        stk_hi stk_lo st_ps st_ok sm_ps sm_max mt_ps mt_ok shift_ok
        s_ps p_exp p_masked p_hi p_lo o_ps o_ok on_ok ot_ps oh_ok ol_ok wo_ps x1_ok
        ctx_ok xs_ps xs_ok xp_ok xpt_ps xph_ok xpl_ok ro_ps x2_ok
        lg_ps g_ready g_exp_ok comb_ok ct_ps ct_ok ct_out cb_in h_ps1 h_ps2 hs_ok hg_ok hc_ok hhi_ok hlo_ok
        w3_done y_ps y_ok out_done""".split()
        names += [f"{n}{i}" for n in ("ln_mv", "ln_rstd", "ln_xn", "xnt_ps", "xn_hi_ok", "xn_lo_ok") for i in range(3)]
        s = {n: sem(n) for n in names}

        block = es.enter_context(nc.Block())

        def head(g, i):
            return 2 * (G * (g // 2) + i) + g % 2

        def halves(a_hi, a_lo, b_hi, b_lo):
            return ((a_hi, b_hi), (a_hi, b_lo), (a_lo, b_hi))

        UPW = FT * P * KC // 512
        CB = sum(1 for e in range(E) for r in range(e * I, (e + 1) * I) if r == e * I or r % P == 0)

        PERIOD = 36.0
        START = {
            "ln1": 0, "ln1n": 1, "xt": 2, "v": 5, "qk0": 6, "vm": 7, "qk1": 8, "sh0": 9, "tr0": 11, "sh1": 12, "tr1": 14,
            "m0": 17, "m1": 19, "m2": 21, "m3": 23, "m4": 25, "m5": 27, "mt": 29,
            "s0": 33, "s1": 37, "h0": 36.5, "pv0": 41.5, "s2": 42, "h1": 41, "pv1": 46.5, "s3": 47, "h2": 46, "pv2": 51,
            "h3": 51.5, "pv3": 55, "ctx": 44,
            "on": 57, "ot": 60, "wo": 63, "ln2": 66, "ln2n": 68, "t2": 70, "xs": 73, "xc": 76, "pt": 78, "ro": 81,
            "ln3": 84, "ln3n": 86, "t3": 88, "lg": 91, "rk": 93, "ct": 96,
        }
        FFN = 4 * PERIOD + 30.0
        FFN_STEP = 3.9

        def order():
            steps = [(START[n] + PERIOD * b, n, b) for n in START for b in range(B)]
            steps += [(START["s0"] + 4.0 * i, "w12", i) for i in range(2 * UPW)]
            steps += [(START["tr1"] + 2 + PERIOD * (B - 1) + 1.5 * i, "w3", i) for i in range(FT)]
            steps += [(START["pv3"] + PERIOD * (B - 1) + 1, "cb", 0), (FFN + FFN_STEP * FT, "cb", 1)]
            steps += [(FFN + FFN_STEP * m, "ffn", m) for m in range(2 * FT)]
            return [(n, b) for _, n, b in sorted(steps)]

        @block.sync
        def _(sp):
            def load_x(b):
                sp.dma_start(res[:, b * NT:(b + 1) * NT, :],
                             x[b].rearrange("(t p) c -> p t c", p=P)).then_inc(s[f"x_in{b}"], 16)

            def load_ctx(b):
                sp.dma_start(ctx_raw[:], ctx[b].rearrange("(t p) c -> p t c", p=P)).then_inc(s["ctx_in"], 16)
                sp.dma_start(ctxt_raw[:], ctx_t[b].rearrange("(k p) n -> p k n", p=P)).then_inc(s["ctxt_in"], 16)

            def load_comb(g):
                sp.wait_ge(s["ct_out"], 16 * (GT // S) * (g + 1))
                for e in range(E):
                    r = e * I
                    while r < (e + 1) * I:
                        j, p0 = divmod(r, P)
                        n = min(P - p0, (e + 1) * I - r)
                        sp.dma_start(comb_b[p0:p0 + n, j, :],
                                     comb_dram[e:e + 1, g * GT:(g + 1) * GT].broadcast_to([n, GT]))\
                            .then_inc(s["cb_in"], 16)
                        r += n

            load_x(0)
            sp.dma_start(wqkv_raw[:], wqkv.rearrange("(k p) n -> p k n", p=P)).then_inc(s["w_in"], 16)
            sp.dma_start(cos_t[:], cos.rearrange("(t p) i -> p t i", p=P)).then_inc(s["tab_in"], 16)
            sp.dma_start(sin_t[:], sin.rearrange("(t p) a i -> p t a i", p=P)).then_inc(s["tab_in"], 16)
            load_x(1)
            sp.dma_start(wo_raw[:], wo.rearrange("(k p) n -> p k n", p=P)).then_inc(s["wo_in"], 16)
            sp.dma_start(gate_raw[:], gate.rearrange("(k p) n -> p k n", p=P)).then_inc(s["gate_in"], 16)
            sp.dma_start(mask_u8[:], mask[None, :, :].broadcast_to([P, B, S])).then_inc(s["mask_in"], 16)
            for part, b in order():
                if part == "mt":
                    sp.wait_ge(s["mt_ok"], b + 1)
                    for par in range(2):
                        sp.dma_start(q_t[SLOT * par + KROWS:SLOT * par + KROWS + 1, b % 2, :, :].bitcast(F32),
                                     negm_t[PAIRS * par:PAIRS * (par + 1), :, :].bitcast(F32))\
                            .then_inc(s["shift_ok"], 16)
                elif part == "ln1" and b == 0:
                    load_x(2)
                    load_x(3)
                    load_ctx(0)
                    sp.dma_start(w1_raw[:], w1.rearrange("(k p) n -> p k n", p=P)).then_inc(s["w1_in"], 16)
                    sp.dma_start(w2_raw[:], w2.rearrange("(k p) n -> p k n", p=P)).then_inc(s["w2_in"], 16)
                elif part == "ro" and b + 1 < B:
                    sp.wait_ge(s["ro_ps"], NT * (b + 1))
                    load_ctx(b + 1)
                elif part == "ct":
                    sp.wait_ge(s["ct_ok"], b + 1)
                    sp.dma_start(comb_dram[:, b * S:(b + 1) * S], comb_t[:].rearrange("e t p -> e (t p)"))\
                        .then_inc(s["ct_out"], 16)
                elif part == "cb":
                    if b:
                        sp.wait_ge(s["hc_ok"], FT)
                    else:
                        sp.wait_ge(s["s_ps"], 3 * NG * B)
                        sp.wait_ge(s["o_ps"], NG * B)
                    load_comb(b)
                elif part == "w3" and b == 0:
                    sp.wait_ge(s["st_ps"], 4 * NT * B)
                    sp.dma_start(w3_raw[:], w3.rearrange("(f p) c -> p f c", p=P)).then_inc(s["w3_in"], 16)
            for t in range(B * NT):
                sp.wait_ge(s["y_ok"], t + 1)
                sp.dma_start(out[t // NT, (t % NT) * P:(t % NT + 1) * P, :], res[:, t, :]).then_inc(s["out_done"], 16)
            sp.wait_ge(s["out_done"], 16 * B * NT)

        @block.gpsimd
        def _(eng):
            chain = [0]

            def link(ins):
                chain[0] += 1
                ins.then_inc(s["pool_chain"], 1)
                eng.wait_ge(s["pool_chain"], chain[0])

            def split(raw, hi, lo, ok):
                link(eng.tensor_scalar(hi, raw, 1.0, 0.0, ALU.mult, ALU.add))
                eng.tensor_tensor(lo, raw, hi.bitcast(F32), ALU.subtract).then_inc(ok, 1)

            eng.memset(pw[:], -0.5)
            eng.memset(ident_b[:], 0.0)
            eng.memset(causal_b[:], 0.0)
            eng.memset(earlier[:], 1.0)
            link(eng.memset(ident[:], 0.0))
            eng.affine_select(out=ident[:], in_=ident[:], compare_op=ALU.not_equal, fill=1.0, base=0,
                              pattern=[[-1, P]], channel_multiplier=1).then_inc(s["const"], 1)

            def ln_rstd(n, b):
                eng.wait_ge(s[f"ln_mv{n}"], b + 1)
                link(eng.tensor_scalar(vare[:, n, :], mv[:, n, :, 1], EPS, None, ALU.add))
                eng.tensor_tensor(rstd[:, n, :], vare[:, n, :], pw[:], ALU.pow).then_inc(s[f"ln_rstd{n}"], 1)

            def up_weights(i):
                name = ("w1", "w2")[i // UPW]
                raw, hi, lo = ((w1_raw, w1_hi, w1_lo), (w2_raw, w2_hi, w2_lo))[i // UPW]
                if i % UPW == 0:
                    eng.wait_ge(s[name + "_in"], 16)
                raw, hi, lo = (v[:].rearrange("p k n -> p (k n)")[:, i % UPW * 512:(i % UPW + 1) * 512]
                               for v in (raw, hi, lo))
                split(raw, hi, lo, s[name + "_ok"])

            for part, b in order():
                if part == "ln1":
                    ln_rstd(0, b)
                    if b == 0:
                        eng.affine_select(out=ident_b[:], in_=ident_b[:], compare_op=ALU.not_equal, fill=1.0, base=0,
                                          pattern=[[-1, P]], channel_multiplier=1)
                        eng.affine_select(out=earlier[:], in_=earlier[:], compare_op=ALU.is_gt, fill=0.0, base=0,
                                          pattern=[[1, E], [-1, E]], channel_multiplier=0)
                        eng.affine_select(out=causal_b[:], in_=causal_b[:], compare_op=ALU.is_ge, fill=NEG, base=0,
                                          pattern=[[-1, P]], channel_multiplier=1).then_inc(s["const"], 1)
                elif part in ("qk0", "qk1"):
                    n = NT * b + int(part[-1])
                    eng.wait_ge(s["rope_ok"], n + 1)
                    if n >= 2:
                        eng.wait_ge(s["stk_hi"], n - 1)
                        eng.wait_ge(s["stk_lo"], n - 1)
                    eng.tensor_tensor(rot[:, n % 2].rearrange("p g (a i) -> p a g i", a=2), rope_c[:], rope_s[:], ALU.add)\
                        .then_inc(s["rot_ok"], 1)
                elif part in ("sh0", "sh1"):
                    n = NT * b + int(part[-1])
                    eng.wait_ge(s["stk_hi"], n + 1)
                    eng.tensor_tensor(stk[:, 0:H, DH:2 * DH], rot[:, n % 2, 0:H, :], stk[:, 0:H, 0:DH].bitcast(F32),
                                      ALU.subtract)
                    eng.tensor_tensor(stk[:, H:2 * H, 2 * DH:3 * DH], rot[:, n % 2, H:2 * H, :],
                                      stk[:, H:2 * H, 0:DH].bitcast(F32), ALU.subtract).then_inc(s["stk_lo"], 1)
                elif part == "m0" and b == 0:
                    eng.wait_ge(s["wo_in"], 16)
                    split(wo_raw[:], wo_hi[:], wo_lo[:], s["wo_ok"])
                    eng.wait_ge(s["gate_in"], 16)
                    split(gate_raw[:], gate_hi[:], gate_lo[:], s["gate_ok"])
                    eng.wait_ge(s["mask_in"], 16)
                    eng.tensor_scalar(mask_add[:], mask_u8[:], -1.0, -NEG, ALU.add, ALU.mult).then_inc(s["mask_ok"], 1)
                elif part in ("s0", "s1", "s2", "s3"):
                    g = int(part[1])
                    n = NG * b + g
                    for i in range(3):
                        eng.wait_ge(s["p_exp"], 3 * n + i + 1)
                        if i < 2:
                            v = prob[:, g % 2, i, :].rearrange("p (h q) -> p h q", h=2)[:, :, 0:P]
                        else:
                            v = prob[:, g % 2, i, :].rearrange("p (h q) -> p h q", h=G)
                        eng.affine_select(out=v, in_=v, compare_op=ALU.is_ge, fill=0.0, base=0,
                                          pattern=[[0, v.shape[1]], [1, P]], channel_multiplier=-1)\
                            .then_inc(s["p_masked"], 1)
                elif part == "ctx":
                    eng.wait_ge(s["ctx_in"], 16 * (b + 1))
                    split(ctx_raw[:], ctx_hi[:], ctx_lo[:], s["ctx_ok"])
                    eng.wait_ge(s["ctxt_in"], 16 * (b + 1))
                    split(ctxt_raw[:], ctxt_hi[:], ctxt_lo[:], s["ctx_ok"])
                elif part == "w12":
                    up_weights(b)
                elif part == "w3":
                    if b == 0:
                        eng.wait_ge(s["w3_in"], 16)
                    j = (b + FE) % FT
                    split(w3_raw[:, j], w3_hi[:, j], w3_lo[:, j], s["w3_ok"])
                elif part == "ln2":
                    ln_rstd(1, b)
                elif part == "ln3":
                    ln_rstd(2, b)

        @block.scalar
        def _(act):
            def halves_of(ps):
                return ps[:].rearrange("p (k t) -> p k t", k=KC)

            def xn_hi_copy(n, b, dst):
                act.wait_ge(s[f"xnt_ps{n}"], b + 1)
                act.copy(dst, halves_of(ps_x1 if n == 0 else ps_tail)).then_inc(s[f"xn_hi_ok{n}"], 1)

            for part, b in order():
                if part == "xt":
                    if b == 0:
                        act.wait_ge(s["w_in"], 16)
                        act.copy(wqkv_hi[:], wqkv_raw[:]).then_inc(s["wqkv_hi_ok"], 1)
                    xn_hi_copy(0, b, xt_hi[:])
                elif part == "v":
                    act.wait_ge(s["v_ps"], b + 1)
                    if b >= 2:
                        act.wait_ge(s["o_ps"], NG * (b - 1))
                    act.copy(v_st[:, b % 2, :, :, 0, 0:DH], ps_x1[:].rearrange("p (t h d) -> p t h d", t=NT, d=DH))\
                        .then_inc(s["v_hi"], 1)
                elif part == "vm":
                    act.wait_ge(s["v_mid"], 2 * b + 1)
                    act.copy(v_st[:, b % 2, :, :, 1, 0:DH], v_r1[:].rearrange("p t (h d) -> p t h d", d=DH))\
                        .then_inc(s["v_hi"], 1)
                elif part in ("sh0", "sh1"):
                    t = int(part[-1])
                    n = NT * b + t
                    act.wait_ge(s["rot_ok"], n + 1)
                    if n:
                        act.wait_ge(s["st_ps"], 4 * n)
                    act.copy(stk[:, :, 0:DH], rot[:, n % 2])
                    act.copy(stk[:, 0:H, 2 * DH:3 * DH], rot[:, n % 2, 0:H, :])
                    act.copy(stk[:, H:2 * H, DH:2 * DH], rot[:, n % 2, H:2 * H, :]).then_inc(s["stk_hi"], 1)
                elif part in ("tr0", "tr1"):
                    t = int(part[-1])
                    n = NT * b + t
                    if b >= 2:
                        act.wait_ge(s["s_ps"], 3 * NG * (b - 1))
                    for c in range(4):
                        act.wait_ge(s["st_ps"], 4 * n + c + 1)
                        dst = q_t if c < 2 else k_t
                        act.copy(dst[:, b % 2, 4 * (c % 2):4 * (c % 2) + 4, t * P:(t + 1) * P],
                                 ps_st[c % 2][:].rearrange("p (j q) -> p j q", j=4)).then_inc(s["st_ok"], 1)
                elif part == "mt":
                    act.wait_ge(s["mt_ps"], b + 1)
                    if b:
                        act.wait_ge(s["shift_ok"], 32 * b)
                    act.copy(negm_t[:], ps_st[0][0:H, 0:S].rearrange("h (t q) -> h t q", t=NT)).then_inc(s["mt_ok"], 1)
                elif part in ("s0", "s1", "s2", "s3"):
                    g = int(part[1])
                    for i in range(3):
                        n = 3 * (NG * b + g) + i
                        act.wait_ge(s["s_ps"], n + 1)
                        if NG * b + g >= 2:
                            act.wait_ge(s["p_lo"], NG * b + g - 1)
                        act.activation(prob[:, g % 2, i, :], ps_s[n % 2][:], ACT.Exp, scale=DH ** -0.5)\
                            .then_inc(s["p_exp"], 1)
                elif part[0] == "h":
                    g = int(part[1])
                    n = NG * b + g
                    act.wait_ge(s["p_masked"], 3 * n + 3)
                    if n >= 2:
                        act.wait_ge(s["o_ps"], n - 1)
                    act.copy(prob_hi[:, g % 2], prob[:, g % 2]).then_inc(s["p_hi"], 1)
                elif part == "ot":
                    act.wait_ge(s["ot_ps"], b + 1)
                    act.copy(tail_hi[:], halves_of(ps_tail)).then_inc(s["oh_ok"], 1)
                elif part == "t2":
                    xn_hi_copy(1, b, tail_hi[:])
                elif part == "xs":
                    act.wait_ge(s["xs_ok"], b + 1)
                    for t in range(NT):
                        act.activation(tail[:, t, :], tail[:, t, :], ACT.Exp, bias=xs_neg[:, t:t + 1],
                                       accum_out=xs_sum[:, t:t + 1]).then_inc(s["xp_ok"], 1)
                elif part == "pt":
                    act.wait_ge(s["xpt_ps"], b + 1)
                    act.copy(tail_hi[:], halves_of(ps_tail)).then_inc(s["xph_ok"], 1)
                elif part == "t3":
                    xn_hi_copy(2, b, x3_hi[:, :, b * S:(b + 1) * S])
                elif part == "lg":
                    act.wait_ge(s["g_ready"], b + 1)
                    act.activation(g_exp[:], g_sub[:], ACT.Exp).then_inc(s["g_exp_ok"], 1)
                elif part == "ct":
                    act.wait_ge(s["ct_ps"], b + 1)
                    if b:
                        act.wait_ge(s["ct_out"], 16 * b)
                    act.copy(comb_t[:], ps_tail[0:E, 0:S].rearrange("e (t q) -> e t q", t=NT)).then_inc(s["ct_ok"], 1)
                elif part == "ffn":
                    m = b
                    act.wait_ge(s["h_ps1"], m + 1)
                    if m >= 2:
                        act.wait_ge(s["hg_ok"], m - 1)
                    act.activation(h_s[:, m % 2], h1_bank[m % 2][:], ACT.Silu).then_inc(s["hs_ok"], 1)
                    act.wait_ge(s["hc_ok"], m + 1)
                    if m >= 2:
                        act.wait_ge(s["w3_done"], m - 1)
                    act.copy(h_hi[:, m % 2], h_c[:, m % 2]).then_inc(s["hhi_ok"], 1)

        @block.vector
        def _(dve):
            chain = [0]

            def link(ins):
                chain[0] += 1
                ins.then_inc(s["dve_chain"], 1)
                dve.wait_ge(s["dve_chain"], chain[0])

            def moments(b, n):
                for t in range(NT):
                    ins = dve.bn_stats(stats[:, n, t, :], res[:, NT * b + t, :])
                link(ins)
                for t in range(NT):
                    ins = dve.bn_aggr(mv[:, n, t, :], stats[:, n, t, :])
                ins.then_inc(s[f"ln_mv{n}"], 1)

            def normalise(b, n):
                dst = tail if n else xn1
                dve.wait_ge(s[f"ln_rstd{n}"], b + 1)
                if n == 0 and b:
                    dve.wait_ge(s["xnt_ps0"], b)
                if n:
                    dve.wait_ge(s["ot_ps" if n == 1 else "xpt_ps"], b + 1)
                for t in range(NT):
                    ins = dve.tensor_scalar(dst[:, t, :], res[:, NT * b + t, :], mv[:, n, t, 0:1],
                                            rstd[:, n, t:t + 1], ALU.subtract, ALU.mult)
                ins.then_inc(s[f"ln_xn{n}"], 1)

            def halves_of(ps):
                return ps[:].rearrange("p (k t) -> p k t", k=KC)

            def xn_lo_sub(n, b, hi, dst):
                dve.wait_ge(s[f"xn_hi_ok{n}"], b + 1)
                dve.tensor_tensor(dst, halves_of(ps_x1 if n == 0 else ps_tail), hi.bitcast(F32), ALU.subtract)\
                    .then_inc(s[f"xn_lo_ok{n}"], 1)

            def maxima(b, f):
                dve.wait_ge(s["sm_ps"], 12 * b + f + 1)
                t, w, j = (0, P, 4 * (f // 2)) if f < 4 else (1, S, 2 * ((f - 4) // 2))
                dve.tensor_reduce(negm[:, t, f % 2, j:j + 512 // w], ps_st[f % 2][:].rearrange("p (j k) -> p j k", k=w),
                                  AX.X, ALU.max, negate=True).then_inc(s["sm_max"], 1)

            dve.memset(stk[:, :, KROWS:SLOT].bitcast(F32), 0.0)
            link(dve.memset(v_st[:, :, :, :, :, DH:VP], 0.0))
            dve.memset(v_st[:, :, :, :, 0, DH:VP], 1.0)
            link(dve.memset(stk[:, H:2 * H, KROWS:KROWS + 1].bitcast(F32), 1.0))

            for part, b in order():
                if part == "ln1":
                    dve.wait_ge(s[f"x_in{b}"], 16)
                    moments(b, 0)
                elif part == "ln1n":
                    normalise(b, 0)
                elif part == "xt":
                    if b == 0:
                        dve.wait_ge(s["wqkv_hi_ok"], 1)
                        dve.tensor_tensor(wqkv_lo[:], wqkv_raw[:], wqkv_hi[:].bitcast(F32), ALU.subtract)\
                            .then_inc(s["wqkv_ok"], 1)
                    xn_lo_sub(0, b, xt_hi[:], xt_lo[:])
                elif part == "v":
                    dve.wait_ge(s["v_hi"], 2 * b + 1)
                    dve.tensor_tensor(v_r1[:].rearrange("p t (h d) -> p t h d", d=DH),
                                      ps_x1[:].rearrange("p (t h d) -> p t h d", t=NT, d=DH),
                                      v_st[:, b % 2, :, :, 0, 0:DH], ALU.subtract).then_inc(s["v_mid"], 1)
                elif part == "vm":
                    dve.wait_ge(s["v_hi"], 2 * b + 2)
                    dve.tensor_tensor(v_st[:, b % 2, :, :, 2, 0:DH], v_r1[:].rearrange("p t (h d) -> p t h d", d=DH),
                                      v_st[:, b % 2, :, :, 1, 0:DH], ALU.subtract).then_inc(s["v_mid"], 1)
                elif part in ("qk0", "qk1"):
                    t = int(part[-1])
                    n = NT * b + t
                    if n == 0:
                        dve.wait_ge(s["tab_in"], 32)
                    dve.wait_ge(s["qk_ps"], n + 1)
                    if n:
                        dve.wait_ge(s["rot_ok"], n)
                    qk = ps_qk[:].rearrange("p (a g i) -> p a g i", a=2, i=DH // 2)
                    dve.tensor_tensor(rope_c[:].rearrange("p a g i -> p (a g) i"), qk.rearrange("p a g i -> p (a g) i"),
                                      cos_t[:, t, None, :].broadcast_to([P, 4 * H, DH // 2]), ALU.mult)
                    for a in range(2):
                        ins = dve.tensor_tensor(rope_s[:, a], qk[:, 1 - a],
                                                sin_t[:, t, a, None, :].broadcast_to([P, 2 * H, DH // 2]), ALU.mult)
                    ins.then_inc(s["rope_ok"], 1)
                elif part[0] == "m" and part != "mt":
                    if b and part == "m0":
                        dve.wait_ge(s["mt_ps"], b)
                    for f in range(2):
                        maxima(b, 2 * int(part[-1]) + f)
                elif part[0] == "h":
                    g = int(part[1])
                    n = NG * b + g
                    dve.wait_ge(s["p_hi"], n + 1)
                    dve.tensor_tensor(prob_lo[:, g % 2], prob[:, g % 2], prob_hi[:, g % 2], ALU.subtract)\
                        .then_inc(s["p_lo"], 1)
                elif part[:2] == "pv":
                    g = int(part[2])
                    n = NG * b + g
                    dve.wait_ge(s["o_ps"], n + 1)
                    reduce_parts(dve, o_sum, ps_out, g, s)
                elif part == "on":
                    dve.wait_ge(s["o_ok"], NT * NG * (b + 1))
                    link(dve.reciprocal(o_rec[:], o_sum[:, :, :, DH:VP]))
                    if b:
                        dve.wait_ge(s["xnt_ps2"], b)
                    dve.tensor_tensor(tail[:].rearrange("p t (h d) -> p t h d", h=H), o_sum[:, :, :, 0:DH], o_rec[:].broadcast_to([P, NT, H, DH]), ALU.mult)\
                        .then_inc(s["on_ok"], 1)
                elif part == "ot":
                    dve.wait_ge(s["oh_ok"], b + 1)
                    dve.tensor_tensor(tail_lo[:], halves_of(ps_tail), tail_hi[:].bitcast(F32), ALU.subtract)\
                        .then_inc(s["ol_ok"], 1)
                elif part == "wo":
                    rb = res[:, NT * b:NT * (b + 1), :]
                    dve.wait_ge(s["wo_ps"], NT * (b + 1))
                    dve.tensor_tensor(rb, ps_tail[:].rearrange("p (t c) -> p t c", t=NT), rb, ALU.add)\
                        .then_inc(s["x1_ok"], 1)
                elif part == "ln2":
                    dve.wait_ge(s["x1_ok"], b + 1)
                    moments(b, 1)
                elif part == "ln2n":
                    normalise(b, 1)
                elif part == "t2":
                    xn_lo_sub(1, b, tail_hi[:], tail_lo[:])
                elif part == "xs":
                    if b == 0:
                        dve.wait_ge(s["mask_in"], 16)
                        link(dve.tensor_reduce(valid[:], mask_u8[:], AX.X, ALU.max))
                        dve.wait_ge(s["mask_ok"], 1)
                    dve.wait_ge(s["xs_ps"], NT * (b + 1))
                    dve.wait_ge(s["xnt_ps1"], b + 1)
                    for t in range(NT):
                        ins = dve.tensor_tensor_reduce(tail[:, t, :], ps_tail[:, t * S:(t + 1) * S], mask_add[:, b, :],
                                                       C ** -0.5, -3e38, ALU.add, ALU.max, xs_max[:, t:t + 1])
                    link(ins)
                    dve.tensor_scalar(xs_neg[:], xs_max[:], -1.0, None, ALU.mult).then_inc(s["xs_ok"], 1)
                elif part == "xc":
                    dve.wait_ge(s["xp_ok"], NT * (b + 1))
                    link(dve.reciprocal(xs_rec[:], xs_sum[:]))
                    link(dve.tensor_scalar(xs_coef[:], xs_rec[:], valid[:, b:b + 1], None, ALU.mult))
                elif part == "pt":
                    dve.wait_ge(s["xph_ok"], b + 1)
                    dve.tensor_tensor(tail_lo[:], halves_of(ps_tail), tail_hi[:].bitcast(F32), ALU.subtract)\
                        .then_inc(s["xpl_ok"], 1)
                elif part == "ro":
                    dve.wait_ge(s["ro_ps"], NT * (b + 1))
                    for t in range(NT):
                        r1 = res[:, NT * b + t, :]
                        dve.scalar_tensor_tensor(out=r1, in0=ps_tail[:, t * C:(t + 1) * C], scalar=xs_coef[:, t:t + 1],
                                                 in1=r1, op0=ALU.mult, op1=ALU.add).then_inc(s["x2_ok"], 1)
                elif part == "ln3":
                    dve.wait_ge(s["x2_ok"], NT * (b + 1))
                    moments(b, 2)
                elif part == "ln3n":
                    normalise(b, 2)
                elif part == "t3":
                    xn_lo_sub(2, b, x3_hi[:, :, b * S:(b + 1) * S], x3_lo[:, :, b * S:(b + 1) * S])
                elif part == "lg":
                    dve.wait_ge(s["lg_ps"], NT * (b + 1))
                    if b == 0:
                        dve.wait_ge(s["const"], 2)
                    lg = ps_tail[:, 0:NT * E].rearrange("p (t e) -> p t e", t=NT)
                    link(dve.tensor_reduce(g_max[:], lg, AX.X, ALU.max))
                    dve.tensor_tensor(g_sub[:], lg, g_max[:, :, None].broadcast_to([P, NT, E]), ALU.subtract)\
                        .then_inc(s["g_ready"], 1)
                elif part == "rk":
                    dve.wait_ge(s["g_exp_ok"], b + 1)
                    link(dve.tensor_reduce(g_sum[:], g_exp[:], AX.X, ALU.add))
                    link(dve.reciprocal(g_rec[:], g_sum[:]))
                    link(dve.tensor_tensor(g_p[:], g_exp[:], g_rec[:, :, None].broadcast_to([P, NT, E]), ALU.mult))
                    for t in range(NT):
                        one = g_p[:, t, :, None].broadcast_to([P, E, E])
                        other = g_p[:, t, None, :].broadcast_to([P, E, E])
                        dve.tensor_tensor(g_gt[:, t], other, one, ALU.is_gt)
                        ins = dve.tensor_tensor(g_eq[:, t], other, one, ALU.is_equal)
                    link(ins)
                    for t in range(NT):
                        ins = dve.tensor_tensor(g_eq[:, t], g_eq[:, t], earlier[:], ALU.mult)
                    link(ins)
                    link(dve.tensor_tensor(g_gt[:], g_gt[:], g_eq[:], ALU.add))
                    link(dve.tensor_reduce(g_rank[:], g_gt[:], AX.X, ALU.add))
                    dve.scalar_tensor_tensor(out=comb[:], in0=g_rank[:], scalar=2.0, in1=g_p[:], op0=ALU.is_lt,
                                             op1=ALU.mult).then_inc(s["comb_ok"], 1)
                elif part == "ffn":
                    m = b
                    g, n = divmod(m, FT)
                    j = (n + FE) % FT
                    dve.wait_ge(s["hs_ok"], m + 1)
                    dve.wait_ge(s["h_ps2"], m + 1)
                    if m >= 2:
                        dve.wait_ge(s["hlo_ok"], m - 1)
                        dve.wait_ge(s["hhi_ok"], m - 1)
                    ins = dve.tensor_tensor(h_c[:, m % 2], h2_bank[m % 2][:], h_s[:, m % 2], ALU.mult)
                    if j >= FE:
                        ins.then_inc(s["hg_ok"], 1)
                        dve.wait_ge(s["hg_ok"], m + 1)
                        dve.sem_inc(s["hc_ok"], 1)
                    else:
                        ins.then_inc(s["hg_ok"], 1)
                        dve.wait_ge(s["cb_in"], 16 * CB * (g + 1))
                        dve.wait_ge(s["hg_ok"], m + 1)
                        dve.tensor_tensor(h_c[:, m % 2], h_c[:, m % 2], comb_b[:, j, :], ALU.mult)\
                            .then_inc(s["hc_ok"], 1)
                    dve.wait_ge(s["hhi_ok"], m + 1)
                    dve.tensor_tensor(h_lo[:, m % 2], h_c[:, m % 2], h_hi[:, m % 2].bitcast(F32), ALU.subtract)\
                        .then_inc(s["hlo_ok"], 1)
                    if n == FT - 1:
                        for t in range(4):
                            dve.wait_ge(s["y_ps"], 2 * g + t // 2 + 1)
                            dve.tensor_tensor(res[:, 4 * g + t, :], y_tile(t), res[:, 4 * g + t, :], ALU.add)\
                                .then_inc(s["y_ok"], 1)

        @block.tensor
        def _(pe):
            def split_product(dst, lhs_hi, lhs_lo, rhs_hi, rhs_lo, kt=KC):
                for k in range(kt):
                    for i, (a, c) in enumerate(halves(lhs_hi, lhs_lo, rhs_hi, rhs_lo)):
                        ins = pe.matmul(dst, a(k), c(k), start=(k == 0 and i == 0), stop=(k == kt - 1 and i == 2))
                return ins

            def transposes(dst, src):
                for k in range(2):
                    for t in range(NT):
                        ins = pe.transpose(dst[:, k * S + t * P:k * S + (t + 1) * P], src(t, k), ident[:])
                return ins

            def head_rows(tensor, b, h, rows):
                r = SLOT * (h % 2)
                return tensor[r:r + rows, b % 2, h // 2, :]

            def product(dst0, dst1, a_hi, a_lo, w_hi, w_lo, name):
                for t, dst in enumerate((dst0, dst1)):
                    tok = slice(t * P, (t + 1) * P)
                    split_product(dst, lambda k: a_hi[:, k, tok], lambda k: a_lo[:, k, tok],
                                  lambda k: w_hi[:, k, :], lambda k: w_lo[:, k, :]).then_inc(s[name], 1)

            def row_maxima_scores(b, f):
                if f >= 2:
                    pe.wait_ge(s["sm_max"], 12 * b + f - 1)
                t = 0 if f < 4 else 1
                keys = P * (t + 1)
                for i in range(512 // keys):
                    h = 2 * (4 * (f // 2) + i if t == 0 else 2 * ((f - 4) // 2) + i) + f % 2
                    dst = ps_st[f % 2][:, i * keys:(i + 1) * keys]
                    pe.matmul(dst, head_rows(q_t, b, h, KROWS)[:, t * P:(t + 1) * P],
                              head_rows(k_t, b, h, KROWS)[:, 0:keys], start=True, stop=True)
                    ins = pe.matmul(dst[:, t * P:keys], ident_b[:], causal_b[:], start=False, stop=True,
                                    skip_group_check=True)
                ins.then_inc(s["sm_ps"], 1)

            def scores(b, g):
                for i in range(3):
                    n = 3 * (NG * b + g) + i
                    if n >= 2:
                        pe.wait_ge(s["p_exp"], n - 1)
                    k0 = 0 if i < 2 else P
                    for c in range(2 if i < 2 else G):
                        h = head(g, 2 * i + c if i < 2 else c)
                        ins = pe.matmul(ps_s[n % 2][:, c * (S - k0):(c + 1) * (S - k0)],
                                        head_rows(k_t, b, h, KROWS + 1)[:, k0:k0 + P],
                                        head_rows(q_t, b, h, KROWS + 1)[:, k0:S], start=True, stop=True)
                    ins.then_inc(s["s_ps"], 1)

            def values(b, g):
                n = NG * b + g
                pe.wait_ge(s["p_hi"], n + 1)
                pe.wait_ge(s["p_lo"], n + 1)
                if g == 0:
                    pe.wait_ge(s["v_mid"], 2 * (b + 1))
                if n:
                    pe.wait_ge(s["o_ok"], NT * n)
                for t in range(NT):
                    for i in range(G):
                        o = (t * G + i) * 3 * VP
                        parts = [(pr, 0, i // 2, (i % 2) * S + t * P) for pr in (prob_hi, prob_lo)]
                        if t:
                            parts += [(pr, 1, 2, i * P) for pr in (prob_hi, prob_lo)]
                        for m, (pr, kt, blk, q0) in enumerate(parts):
                            ins = pe.matmul(ps_out[:, o:o + 3 * VP], pr[:, g % 2, blk, q0:q0 + P],
                                            v_st[:, b % 2, kt, head(g, i)].rearrange("p a d -> p (a d)"),
                                            start=(m == 0), stop=(m == len(parts) - 1))
                ins.then_inc(s["o_ps"], 1)

            def up(m):
                g, n = divmod(m, FT)
                j = (n + FE) % FT
                if m >= 2:
                    pe.wait_ge(s["hg_ok"], m - 1)
                hid = slice(j * P, (j + 1) * P)
                tok = slice(g * GT, (g + 1) * GT)
                for w_hi, w_lo, bk, name in ((w1_hi, w1_lo, h1_bank, "h_ps1"), (w2_hi, w2_lo, h2_bank, "h_ps2")):
                    split_product(bk[m % 2][:], lambda k: w_hi[:, k, hid], lambda k: w_lo[:, k, hid],
                                  lambda k: x3_hi[:, k, tok], lambda k: x3_lo[:, k, tok]).then_inc(s[name], 1)

            def down(m):
                g, n = divmod(m, FT)
                j = (n + FE) % FT
                pe.wait_ge(s["hlo_ok"], m + 1)
                pe.wait_ge(s["hhi_ok"], m + 1)
                if not g:
                    pe.wait_ge(s["w3_ok"], n + 1)
                for t in range(4):
                    if g and n == 0:
                        pe.wait_ge(s["y_ok"], 2 * (t // 2) + 2)
                    tok = slice(t * P, (t + 1) * P)
                    for i, (a, c) in enumerate(halves(h_hi, h_lo, w3_hi, w3_lo)):
                        ins = pe.matmul(y_tile(t), a[:, m % 2, tok], c[:, j, :],
                                        start=(n == 0 and i == 0 and t % 2 == 0), stop=(n == FT - 1 and i == 2),
                                        skip_group_check=True)
                    if n == FT - 1 and t % 2:
                        ins.then_inc(s["y_ps"], 1)
                if n < FT - 1:
                    ins.then_inc(s["w3_done"], 1)
                else:
                    pe.wait_ge(s["y_ps"], 2 * (g + 1))
                    pe.sem_inc(s["w3_done"], 1)

            out_tiles = [ps_tail[:, t * C:(t + 1) * C] for t in range(NT)]
            pe.wait_ge(s["const"], 1)
            for part, b in order():
                if part == "xt":
                    pe.wait_ge(s["ln_xn0"], b + 1)
                    if b:
                        pe.wait_ge(s["v_mid"], 2 * b - 1)
                    transposes(ps_x1, lambda t, k: xn1[:, t, k * P:(k + 1) * P]).then_inc(s["xnt_ps0"], 1)
                elif part == "v":
                    pe.wait_ge(s["xn_lo_ok0"], b + 1)
                    pe.wait_ge(s["wqkv_ok"], 1)
                    for t in range(NT):
                        tok = slice(t * P, (t + 1) * P)
                        ins = split_product(ps_x1[:, t * C:(t + 1) * C], lambda k: xt_hi[:, k, tok],
                                            lambda k: xt_lo[:, k, tok], lambda k: wqkv_hi[:, k, 2 * C:3 * C],
                                            lambda k: wqkv_lo[:, k, 2 * C:3 * C])
                    ins.then_inc(s["v_ps"], 1)
                elif part in ("qk0", "qk1"):
                    t = int(part[-1])
                    tok = slice(t * P, (t + 1) * P)
                    if NT * b + t:
                        pe.wait_ge(s["rope_ok"], NT * b + t)
                    split_product(ps_qk[:], lambda k: xt_hi[:, k, tok], lambda k: xt_lo[:, k, tok],
                                  lambda k: wqkv_hi[:, k, 0:2 * C], lambda k: wqkv_lo[:, k, 0:2 * C])\
                        .then_inc(s["qk_ps"], 1)
                elif part in ("tr0", "tr1"):
                    n = NT * b + int(part[-1])
                    pe.wait_ge(s["stk_lo"], n + 1)
                    if b and part == "tr0":
                        pe.wait_ge(s["mt_ok"], b)
                        pe.wait_ge(s["sm_max"], 12 * b)
                    for c in range(4):
                        if 4 * n + c >= 2:
                            pe.wait_ge(s["st_ok"], 4 * n + c - 1)
                        for j in range(4):
                            h = 8 * c + 2 * j
                            ins = pe.transpose(ps_st[c % 2][:, j * P:(j + 1) * P],
                                               stk[:, h:h + 2, :].bitcast(F32).rearrange("p h r -> p (h r)"), ident[:])
                        ins.then_inc(s["st_ps"], 1)
                elif part[0] == "m" and part != "mt":
                    if part == "m0":
                        pe.wait_ge(s["st_ok"], 4 * NT * (b + 1))
                        if b == 0:
                            pe.wait_ge(s["const"], 2)
                    for f in range(2):
                        row_maxima_scores(b, 2 * int(part[-1]) + f)
                elif part == "mt":
                    pe.wait_ge(s["sm_max"], 12 * (b + 1))
                    for t in range(NT):
                        ins = pe.transpose(ps_st[0][0:H, t * P:(t + 1) * P],
                                           negm[:, t].rearrange("p r j -> p (r j)"), ident[:])
                    ins.then_inc(s["mt_ps"], 1)
                elif part in ("s0", "s1", "s2", "s3"):
                    if part == "s0":
                        pe.wait_ge(s["shift_ok"], 32 * (b + 1))
                    scores(b, int(part[-1]))
                elif part[:2] == "pv":
                    values(b, int(part[-1]))
                elif part in ("ot", "t2", "pt", "t3"):
                    ready, n, done = {"ot": ("on_ok", 1, "ot_ps"), "t2": ("ln_xn1", 1, "xnt_ps1"),
                                      "pt": ("xp_ok", NT, "xpt_ps"), "t3": ("ln_xn2", 1, "xnt_ps2")}[part]
                    pe.wait_ge(s[ready], n * (b + 1))
                    if b and part == "ot":
                        pe.wait_ge(s["ct_ok"], b)
                    transposes(ps_tail, lambda t, k: tail[:, t, k * P:(k + 1) * P]).then_inc(s[done], 1)
                elif part == "wo":
                    pe.wait_ge(s["ol_ok"], b + 1)
                    pe.wait_ge(s["wo_ok"], 1)
                    product(*out_tiles, tail_hi, tail_lo, wo_hi, wo_lo, "wo_ps")
                elif part == "xs":
                    pe.wait_ge(s["xn_lo_ok1"], b + 1)
                    pe.wait_ge(s["ctx_ok"], 2 * (b + 1))
                    product(*out_tiles, tail_hi, tail_lo, ctxt_hi, ctxt_lo, "xs_ps")
                elif part == "ro":
                    pe.wait_ge(s["xpl_ok"], b + 1)
                    product(*out_tiles, tail_hi, tail_lo, ctx_hi, ctx_lo, "ro_ps")
                elif part == "lg":
                    pe.wait_ge(s["xn_lo_ok2"], b + 1)
                    pe.wait_ge(s["gate_ok"], 1)
                    for t in range(NT):
                        tok = slice((NT * b + t) * P, (NT * b + t + 1) * P)
                        split_product(ps_tail[:, t * E:(t + 1) * E], lambda k: x3_hi[:, k, tok],
                                      lambda k: x3_lo[:, k, tok], lambda k: gate_hi[:, k, :],
                                      lambda k: gate_lo[:, k, :]).then_inc(s["lg_ps"], 1)
                elif part == "ct":
                    pe.wait_ge(s["comb_ok"], b + 1)
                    for t in range(NT):
                        ins = pe.transpose(ps_tail[0:E, t * P:(t + 1) * P], comb[:, t, :], ident[:])
                    ins.then_inc(s["ct_ps"], 1)
                elif part == "ffn":
                    m = b
                    g, n = divmod(m, FT)
                    if m == 0:
                        pe.wait_ge(s["w1_ok"], UPW)
                        pe.wait_ge(s["w2_ok"], UPW)
                        pe.wait_ge(s["mt_ok"], B)
                        pe.wait_ge(s["p_exp"], 3 * NG * B)
                        pe.wait_ge(s["xn_lo_ok2"], GT // S)
                    if m == FT:
                        pe.wait_ge(s["xn_lo_ok2"], B)
                    up(m)
                    if m:
                        down(m - 1)
                    if m == 2 * FT - 1:
                        down(m)


def reduce_parts(dve, o_sum, ps_out, g, s):
    for t in range(NT):
        w = G * 3 * VP
        dve.tensor_reduce(o_sum[:, t].rearrange("p (j r) d -> p j r d", r=2)[:, G * (g // 2):G * (g // 2) + G, g % 2, :],
                          ps_out[:, t * w:(t + 1) * w].rearrange("p (h a d) -> p h d a", h=G, a=3), AX.X, ALU.add)\
            .then_inc(s["o_ok"], 1)


def kernel(**inputs):
    import numpy as np
    import concourse.bacc as bacc
    from concourse.bass_utils import run_bass_kernel_spmd

    a = {k: np.asarray(v) for k, v in inputs.items()}
    order = np.arange(C).reshape(H, DH // 2, 2).transpose(2, 0, 1).reshape(2, -1)
    columns = np.concatenate([order[0], C + order[0], order[1], C + order[1], 2 * C + np.arange(C)])
    hidden = FT * P

    def up(w, shared):
        return np.concatenate([w.reshape(E * I, C), shared, np.zeros((hidden - E * I - IS, C), w.dtype)]).T

    w3 = a["L0_ffn_w3"]
    down = np.concatenate([w3.transpose(0, 2, 1).reshape(E * I, C), a["L0_ffn_sw3"].T,
                           np.zeros((hidden - E * I - IS, C), w3.dtype)])
    inv = (1.0 / np.float32(10000.0) ** (2.0 * np.arange(DH // 2, dtype=np.float32) / DH)).astype(np.float32)
    angle = np.outer(np.arange(S, dtype=np.float32), inv).astype(np.float32)
    arrays = {
        "x": a["x"], "ctx": a["ctx_2048"], "ctx_t": a["ctx_2048"].transpose(0, 2, 1), "mask": a["mask_BxS2_bk0"],
        "wqkv": a["L0_attn_Wqkv"][:, columns], "wo": a["L0_attn_Wo"], "gate": a["L0_ffn_gate_w"].T,
        "w1": up(a["L0_ffn_w1"], a["L0_ffn_sw1"]), "w2": up(a["L0_ffn_w2"], a["L0_ffn_sw2"]), "w3": down,
        "cos": np.cos(angle), "sin": np.stack([-np.sin(angle), np.sin(angle)], axis=1),
    }
    arrays = {k: np.ascontiguousarray(v) for k, v in arrays.items()}
    nc = bacc.Bacc("TRN2", target_bir_lowering=False, num_devices=1)
    args = [nc.dram_tensor(k, v.shape, mybir.dt.from_np(v.dtype), kind="ExternalInput").ap() for k, v in arrays.items()]
    out = nc.dram_tensor("out", (B, S, C), F32, kind="ExternalOutput").ap()
    decoder_layer(nc, *args, out)
    r = run_bass_kernel_spmd(nc, [arrays], core_ids=[0])
    return r.results[0]["out"]
```

```python
from contextlib import ExitStack

import concourse.bass as bass
from concourse import mybir

ALU = mybir.AluOpType
ACT = mybir.ActivationFunctionType
AX = mybir.AxisListType
F32 = mybir.dt.float32
F32R = mybir.dt.float32r
BF16 = mybir.dt.bfloat16
FP16 = mybir.dt.float16
U8 = mybir.dt.uint8

P = 128
B, S, C = 4, 256, 256
NT = S // P
KC = C // P
H, DH = 16, 16
PAIRS = H // 2
SLOT = 64
KROWS = 3 * DH
G = 4
NG = H // G
VP = DH + 1
E, I, IS = 8, 176, 352
FT = 14
FE = E * I // P
GT = 512
EPS = 1e-5
NEG = -1e30


ORDER = {
    "SP": """
        ln1.0 mt.0 mt.1 ro.0 mt.2 ct.0 w3.0 ro.1 mt.3 ct.1 ro.2 cb.0 ct.2 ct.3 cb.1 y.0 y.1
    """,
    "POOL": """
        ln1.0 ctx.0 w12.0 w12.1 qk.0 w12.2 sh.0 qk.1 ln1.1 w12.3 w12.4 w12.5 sh.1 tr.7 w12.6 w12.7 w12.8 w12.9
        qk.2 w12.10 w12.11 qk.3 w12.12 w12.13 ln1.2 sh.2 s.0 s.1 s.2 s.3 s.4 s.5 sh.3 s.6 s.7 s.8 s.9 s.10 s.11
        h.3 qk.4 sh.4 s.12 s.13 qk.5 ln1.3 s.14 s.15 s.16 s.17 ln2.0 s.18 sh.5 s.19 s.20 s.21 s.22 s.23 h.7
        ln3.0 ctx.1 qk.6 sh.6 s.24 s.25 s.26 s.27 qk.7 s.28 s.29 s.30 ln2.1 sh.7 s.31 s.32 s.33 s.34 s.35 h.11
        w3.0 ln3.1 ctx.2 w3.1 w3.2 w3.3 w3.4 w3.5 w3.6 w3.7 w3.8 s.36 s.37 w3.9 s.38 w3.10 w3.11 w3.12 s.39 s.40
        w3.13 s.41 s.42 ln2.2 s.43 s.44 s.45 s.46 s.47 h.15 ln3.2 ctx.3 ln2.3 ln3.3
    """,
    "ACT": """
        ln1n.0 xt.0 v.0 w12.0 w12.1 vm.0 w12.2 w12.3 w12.4 w12.5 w12.6 sh.0 w12.7 w12.8 w12.9 w12.10 w12.11 tr.0
        w12.12 tr.1 ln1n.1 tr.2 tr.3 sh.1 xt.1 w12.13 v.1 tr.4 vm.1 tr.5 tr.6 tr.7 ln1n.2 mt.0 sh.2 xt.2 s.0 s.1
        tr.8 s.2 s.3 tr.9 h.0 s.4 s.5 tr.10 tr.11 sh.3 s.6 h.1 s.7 tr.12 s.8 tr.13 s.9 tr.14 h.2 tr.15 s.10 s.11
        h.3 v.2 mt.1 vm.2 sh.4 ot.0 s.12 s.13 s.14 s.15 tr.16 s.16 s.17 tr.17 tr.18 h.4 h.5 ln2n.0 s.18 tr.19
        sh.5 t2.0 s.19 s.20 ln1n.3 s.21 h.6 tr.20 tr.21 xs.0 tr.22 tr.23 s.22 s.23 pt.0 xt.3 h.7 v.3 ln3n.0 vm.3
        t3.0 mt.2 sh.6 lg.0 s.24 s.25 tr.24 ct.0 s.26 s.27 ot.1 h.8 s.28 s.29 tr.25 tr.26 s.30 h.9 tr.27 sh.7
        ln2n.1 s.31 s.32 t2.1 h.10 tr.28 tr.29 s.33 tr.30 tr.31 xs.1 s.34 s.35 pt.1 h.11 w3.0 w3.1 w3.2 w3.3
        w3.4 w3.5 w3.6 w3.7 w3.8 w3.9 w3.10 w3.11 w3.12 w3.13 ln3n.1 t3.1 mt.3 lg.1 s.36 s.37 ct.1 s.38 ot.2
        h.12 s.39 s.40 s.41 s.42 h.13 s.43 ln2n.2 s.44 s.45 t2.2 h.14 s.46 s.47 h.15 xs.2 up.0 pt.2 up.1 dn.0
        dn.1 up.2 up.3 ln3n.2 dn.2 t3.2 up.4 lg.2 dn.3 up.5 dn.4 up.6 ct.2 dn.5 ot.3 up.7 dn.6 up.8 ln2n.3 dn.7
        t2.3 up.9 xs.3 dn.8 up.10 pt.3 dn.9 up.11 dn.10 up.12 ln3n.3 dn.11 t3.3 up.13 lg.3 dn.12 up.14 dn.13
        ct.3 up.15 dn.14 up.16 dn.15 up.17 dn.16 up.18 dn.17 dn.18 up.19 up.20 dn.19 up.21 dn.20 up.22 dn.21
        up.23 dn.22 up.24 dn.23 up.25 dn.24 up.26 dn.25 up.27 dn.26 dn.27
    """,
    "DVE": """
        ln1.0 xt.0 v.0 qk.0 vm.0 qk.1 ln1.1 xt.1 v.1 qk.2 m.0 m.1 vm.1 qk.3 m.2 m.3 m.4 m.5 m.6 m.7 m.8 ln1.2
        m.9 m.10 m.11 xt.2 h.0 pv.0 h.1 pv.1 h.2 m.12 m.13 pv.2 m.14 m.15 m.16 m.17 m.18 m.19 m.20 pv.3 m.21
        m.22 m.23 on.0 v.2 qk.4 vm.2 ot.0 qk.5 ln1.3 wo.0 ln2.0 h.4 h.5 pv.4 t2.0 pv.5 xs.0 h.6 xc.0 pv.6 m.24
        pt.0 m.25 m.26 xt.3 ro.0 m.27 m.28 ln3.0 m.29 m.30 pv.7 v.3 m.31 m.32 m.33 m.34 m.35 t3.0 qk.6 vm.3 lg.0
        rk.0 on.1 qk.7 ot.1 h.8 wo.1 ln2.1 pv.8 h.9 pv.9 t2.1 h.10 xs.1 pv.10 m.36 xc.1 m.37 pt.1 m.38 m.39 ro.1
        m.40 m.41 ln3.1 m.42 m.43 m.44 m.45 pv.11 m.46 m.47 t3.1 lg.1 rk.1 on.2 ot.2 h.12 wo.2 ln2.2 pv.12 h.13
        t2.2 pv.13 h.14 xs.2 xc.2 pv.14 up.0 pt.2 dn.0 up.1 ro.2 pv.15 ln3.2 dn.1 up.2 dn.2 t3.2 up.3 lg.2 up.4
        rk.2 on.3 dn.3 dn.4 up.5 up.6 ot.3 dn.5 up.7 wo.3 ln2.3 dn.6 up.8 dn.7 t2.3 up.9 xs.3 xc.3 dn.8 up.10
        pt.3 dn.9 up.11 ro.3 ln3.3 dn.10 up.12 dn.11 t3.3 up.13 lg.3 rk.3 dn.12 up.14 dn.13 up.15 dn.14 up.16
        y.0 dn.15 dn.16 up.17 up.18 dn.17 dn.18 up.19 up.20 dn.19 up.21 dn.20 up.22 dn.21 up.23 dn.22 up.24
        dn.23 up.25 dn.24 up.26 dn.25 up.27 dn.26 dn.27 y.1
    """,
    "PE": """
        xt.0 v.0 qk.0 qk.1 tr.0 tr.1 tr.2 tr.3 xt.1 v.1 tr.4 tr.5 tr.6 tr.7 qk.2 m.0 m.1 qk.3 m.2 m.3 m.4 m.5
        m.6 m.7 m.8 m.9 m.10 m.11 mt.0 xt.2 s.0 s.1 tr.8 tr.9 s.2 s.3 tr.10 s.4 s.5 tr.11 v.2 s.6 qk.4 s.7 pv.0
        s.8 tr.12 tr.13 s.9 tr.14 s.10 pv.1 tr.15 s.11 m.12 m.13 pv.2 m.14 m.15 m.16 m.17 m.18 m.19 m.20 pv.3
        m.21 m.22 m.23 mt.1 ot.0 s.12 s.13 qk.5 wo.0 s.14 s.15 tr.16 tr.17 s.16 s.17 tr.18 s.18 s.19 tr.19 pv.4
        t2.0 s.20 pv.5 s.21 xs.0 tr.20 tr.21 s.22 s.23 tr.22 tr.23 xt.3 pt.0 pv.6 m.24 m.25 m.26 ro.0 m.27 m.28
        v.3 m.29 m.30 pv.7 qk.6 m.31 m.32 m.33 m.34 t3.0 m.35 mt.2 lg.0 qk.7 s.24 s.25 tr.24 ct.0 s.26 s.27
        tr.25 ot.1 s.28 tr.26 s.29 wo.1 s.30 s.31 tr.27 pv.8 s.32 pv.9 t2.1 tr.28 s.33 tr.29 xs.1 tr.30 s.34
        tr.31 s.35 pv.10 m.36 m.37 pt.1 m.38 m.39 ro.1 m.40 m.41 m.42 m.43 pv.11 m.44 m.45 m.46 m.47 t3.1 mt.3
        lg.1 s.36 s.37 ct.1 s.38 ot.2 s.39 s.40 wo.2 s.41 s.42 pv.12 s.43 s.44 s.45 t2.2 s.46 s.47 pv.13 xs.2
        up.0 pv.14 pt.2 up.1 ro.2 pv.15 up.2 up.3 dn.0 t3.2 up.4 lg.2 dn.1 up.5 dn.2 up.6 ct.2 dn.3 ot.3 up.7
        wo.3 dn.4 up.8 dn.5 t2.3 up.9 xs.3 dn.6 up.10 pt.3 dn.7 up.11 ro.3 dn.8 up.12 dn.9 t3.3 up.13 lg.3 dn.10
        up.14 dn.11 ct.3 up.15 dn.12 up.16 dn.13 up.17 dn.14 up.18 dn.15 dn.16 up.19 up.20 dn.17 up.21 dn.18
        up.22 dn.19 up.23 dn.20 up.24 dn.21 up.25 dn.22 up.26 dn.23 up.27 dn.24 dn.25 dn.26 dn.27
    """,
}


def decoder_layer(nc, x, ctx, ctx_t, mask, wqkv, wo, gate, w1, w2, w3, cos, sin, out):
    with ExitStack() as es:
        def sb(name, shape, dt=F32):
            return es.enter_context(nc.sbuf_tensor(name, shape, dt))

        def raw_and_lo(alloc, name, shape):
            with nc.sbuf_tensor(name + "_raw", shape, F32) as raw:
                pass
            return raw, alloc(name + "_lo", shape, F32R)

        attention = ExitStack()

        def sa(name, shape, dt=F32):
            return attention.enter_context(nc.sbuf_tensor(name, shape, dt))

        def sem(name):
            return es.enter_context(nc.semaphore(name))

        comb_dram = nc.dram_tensor("comb_dram", (E, B * S), F32, kind="Internal").ap()

        res = sb("res", [P, B * NT, C])
        gate_raw, gate_lo = raw_and_lo(sb, "gate", [P, KC, E])
        gate_hi = sb("gate_hi", [P, KC, E], F32R)
        w1_raw, w1_lo = raw_and_lo(sb, "w1", [P, KC, FT * P])
        w2_raw, w2_lo = raw_and_lo(sb, "w2", [P, KC, FT * P])
        w1_hi = sb("w1_hi", [P, KC, FT * P], F32R)
        w2_hi = sb("w2_hi", [P, KC, FT * P], F32R)
        cos_t = sb("cos_t", [P, NT, DH // 2])
        sin_t = sb("sin_t", [P, NT, 2, DH // 2])
        mask_u8 = sb("mask_u8", [P, B, S], U8)
        mask_add = sb("mask_add", [P, B, S], BF16)
        valid = sb("valid", [P, B])
        ident = sb("ident", [P, P])
        ident_b = sb("ident_b", [P, P], BF16)
        causal_b = sb("causal_b", [P, P], BF16)
        earlier = sb("earlier", [P, E, E])
        pw = sb("pw", [P, 2])
        stats = sb("stats", [P, 3, NT, 6])
        mv = sb("mv", [P, 3, NT, 2])
        vare = sb("vare", [P, 3, NT])
        rstd = sb("rstd", [P, 3, NT])
        shift = sb("shift", [P, 3, NT])
        x3_hi = sb("x3_hi", [P, KC, B * S], F32R)
        x3_lo = sb("x3_lo", [P, KC, B * S], F32R)
        xs_max = sb("xs_max", [P, NT])
        xs_neg = sb("xs_neg", [P, NT])
        xs_sum = sb("xs_sum", [P, NT])
        xs_rec = sb("xs_rec", [P, NT])
        xs_coef = sb("xs_coef", [P, NT])
        g_max = sb("g_max", [P, NT])
        g_sub = sb("g_sub", [P, NT, E])
        g_exp = sb("g_exp", [P, NT, E])
        g_sum = sb("g_sum", [P, NT])
        g_rec = sb("g_rec", [P, NT])
        g_p = sb("g_p", [P, NT, E])
        g_gt = sb("g_gt", [P, NT, E, E])
        g_eq = sb("g_eq", [P, NT, E, E])
        g_rank = sb("g_rank", [P, NT, E])
        comb = sb("comb", [P, NT, E])
        comb_t = sb("comb_t", [E, NT, P])

        o_sum = sb("o_sum", [P, NT, H, VP])
        o_rec = sb("o_rec", [P, NT, H, 1])
        tail = sb("tail", [P, NT, C])
        tail_hi = sb("tail_hi", [P, KC, S], F32R)
        tail_lo = sb("tail_lo", [P, KC, S], F32R)
        wo_raw, wo_lo = raw_and_lo(sb, "wo", [P, KC, C])
        wo_hi = sb("wo_hi", [P, KC, C], F32R)
        ctx_raw, ctx_lo = raw_and_lo(sb, "ctx", [P, NT, C])
        ctx_hi = sb("ctx_hi", [P, NT, C], F32R)
        ctxt_raw, ctxt_lo = raw_and_lo(sb, "ctxt", [P, KC, S])
        ctxt_hi = sb("ctxt_hi", [P, KC, S], F32R)
        wqkv_raw, wqkv_lo = raw_and_lo(sa, "wqkv", [P, KC, 3 * C])
        wqkv_hi = sa("wqkv_hi", [P, KC, 3 * C], F32R)
        xn1 = sa("xn1", [P, NT, C])
        xt_hi = sa("xt_hi", [P, KC, S], F32R)
        xt_lo = sa("xt_lo", [P, KC, S], F32R)
        rope_c = sa("rope_c", [P, 2, 2 * H, DH // 2])
        rope_s = sa("rope_s", [P, 2, 2 * H, DH // 2])
        rot = sa("rot", [P, 2, 2 * H, DH])
        stk = sa("stk", [P, 2 * H, SLOT], F32R)
        q_t = sa("q_t", [P, 2, PAIRS, S], F32R)
        k_t = sa("k_t", [P, 2, PAIRS, S], F32R)
        v_r1 = sa("v_r1", [P, NT, C])
        negm = sa("negm", [P, NT, 2, PAIRS])
        negm_t = sa("negm_t", [H, NT, P], F32R)
        v_st = sa("v_st", [P, 2, NT, H, 3, VP], BF16)
        prob = sa("prob", [P, 2, 3, 512])
        prob_hi = sa("prob_hi", [P, 2, 3, 512], FP16)
        prob_lo = sa("prob_lo", [P, 2, 3, 512], FP16)
        attention.close()
        w3_raw, w3_lo = raw_and_lo(sb, "w3", [P, FT, C])
        w3_hi = sb("w3_hi", [P, FT, C], F32R)
        h_s = sb("h_s", [P, 2, GT])
        h_c = sb("h_c", [P, 2, GT])
        h_hi = sb("h_hi", [P, 2, GT], F32R)
        h_lo = sb("h_lo", [P, 2, GT], F32R)
        comb_b = sb("comb_b", [P, FE, GT])

        bank = [es.enter_context(nc.psum_tensor(f"bank{i}", [P, 512], F32)) for i in range(8)]
        ps_x1, ps_qk, ps_tail, ps_out = bank[0], bank[1], bank[2], bank[7]
        ps_st = [bank[3], bank[4]]
        ps_s = [bank[5], bank[6]]
        h1_bank, h2_bank = [bank[3], bank[4]], [bank[5], bank[6]]

        def y_tile(t):
            return bank[t // 2][:, t % 2 * C:(t % 2 + 1) * C]

        names = """x_in0 x_in1 x_in2 x_in3 w_in wo_in gate_in w1_in w2_in w3_in tab_in mask_in ctx_in ctxt_in
        const pool_chain dve_chain wqkv_hi_ok wqkv_ok wo_ok gate_ok w12_hi_ok w12_ok w3_hi_ok w3_ok mask_ok
        qk_ps v_ps rope_ok rot_ok v_hi v_mid
        stk_hi stk_lo st_ps st_ok sm_ps sm_max mt_ps mt_ok shift_ok
        s_ps p_exp p_masked p_hi p_lo p_lo_last o_ps o_ok on_ok ot_ps oh_ok ol_ok wo_ps x1_ok
        valid_ok ctx_ok xs_ps xs_ok xp_ok xpt_ps xph_ok xpl_ok ro_ps x2_ok
        lg_ps g_ready g_exp_ok comb_ok ct_ps ct_ok ct_out cb_in h_ps1 h_ps2 hs_ok hg_ok hc_ok hhi_ok hlo_ok
        w3_done y_ps y_ok out_done""".split()
        names += [f"{n}{i}" for n in ("ln_mv", "ln_rstd", "ln_xn", "xnt_ps", "xn_hi_ok", "xn_lo_ok") for i in range(3)]
        s = {n: sem(n) for n in names}

        block = es.enter_context(nc.Block())

        def head(g, i):
            return 2 * (G * (g // 2) + i) + g % 2

        def wait_p_lo(engine, n):
            if n % NG == NG - 1:
                engine.wait_ge(s["p_lo_last"], n // NG + 1)
            else:
                engine.wait_ge(s["p_lo"], n - n // NG + 1)

        def up_weights(i):
            parts = ((w1_raw, w1_hi, w1_lo), (w2_raw, w2_hi, w2_lo))[i // UPW]
            return [v[:].rearrange("p k n -> p (k n)")[:, i % UPW * 512:(i % UPW + 1) * 512] for v in parts]

        def halves(a_hi, a_lo, b_hi, b_lo):
            return ((a_hi, b_hi), (a_hi, b_lo), (a_lo, b_hi))

        UPW = FT * P * KC // 512
        CB = sum(1 for e in range(E) for r in range(e * I, (e + 1) * I) if r == e * I or r % P == 0)

        def steps(engine):
            for step in ORDER[engine].split():
                name, number = step.split(".")
                yield name, int(number)

        @block.sync
        def _(sp):
            def load_x(b):
                sp.dma_start(res[:, b * NT:(b + 1) * NT, :],
                             x[b].rearrange("(t p) c -> p t c", p=P)).then_inc(s[f"x_in{b}"], 16)

            def load_ctx(b):
                sp.dma_start(ctx_raw[:], ctx[b].rearrange("(t p) c -> p t c", p=P)).then_inc(s["ctx_in"], 16)
                sp.dma_start(ctxt_raw[:], ctx_t[b].rearrange("(k p) n -> p k n", p=P)).then_inc(s["ctxt_in"], 16)

            def load_comb(g):
                sp.wait_ge(s["ct_out"], 16 * (GT // S) * (g + 1))
                for e in range(E):
                    r = e * I
                    while r < (e + 1) * I:
                        j, p0 = divmod(r, P)
                        n = min(P - p0, (e + 1) * I - r)
                        sp.dma_start(comb_b[p0:p0 + n, j, :],
                                     comb_dram[e:e + 1, g * GT:(g + 1) * GT].broadcast_to([n, GT]))\
                            .then_inc(s["cb_in"], 16)
                        r += n

            load_x(0)
            sp.dma_start(wqkv_raw[:], wqkv.rearrange("(k p) n -> p k n", p=P)).then_inc(s["w_in"], 16)
            sp.dma_start(cos_t[:], cos.rearrange("(t p) i -> p t i", p=P)).then_inc(s["tab_in"], 16)
            sp.dma_start(sin_t[:], sin.rearrange("(t p) a i -> p t a i", p=P)).then_inc(s["tab_in"], 16)
            load_x(1)
            sp.dma_start(wo_raw[:], wo.rearrange("(k p) n -> p k n", p=P)).then_inc(s["wo_in"], 16)
            sp.dma_start(gate_raw[:], gate.rearrange("(k p) n -> p k n", p=P)).then_inc(s["gate_in"], 16)
            sp.dma_start(mask_u8[:], mask[None, :, :].broadcast_to([P, B, S])).then_inc(s["mask_in"], 16)
            for part, b in steps("SP"):
                if part == "mt":
                    sp.wait_ge(s["mt_ok"], b + 1)
                    for par in range(2):
                        sp.dma_start(q_t[SLOT * par + KROWS:SLOT * par + KROWS + 1, b % 2, :, :].bitcast(F32),
                                     negm_t[PAIRS * par:PAIRS * (par + 1), :, :].bitcast(F32))\
                            .then_inc(s["shift_ok"], 16)
                elif part == "ln1" and b == 0:
                    load_x(2)
                    load_x(3)
                    load_ctx(0)
                    sp.dma_start(w1_raw[:], w1.rearrange("(k p) n -> p k n", p=P)).then_inc(s["w1_in"], 16)
                    sp.dma_start(w2_raw[:], w2.rearrange("(k p) n -> p k n", p=P)).then_inc(s["w2_in"], 16)
                elif part == "ro" and b + 1 < B:
                    sp.wait_ge(s["ro_ps"], NT * (b + 1))
                    load_ctx(b + 1)
                elif part == "ct":
                    sp.wait_ge(s["ct_ok"], b + 1)
                    sp.dma_start(comb_dram[:, b * S:(b + 1) * S], comb_t[:].rearrange("e t p -> e (t p)"))\
                        .then_inc(s["ct_out"], 16)
                elif part == "cb":
                    if b:
                        sp.wait_ge(s["hc_ok"], FT)
                    else:
                        sp.wait_ge(s["s_ps"], 3 * NG * B)
                        sp.wait_ge(s["o_ps"], NG * B)
                    load_comb(b)
                elif part == "y":
                    for t in range(4 * b, 4 * b + 4):
                        sp.wait_ge(s["y_ok"], t + 1)
                        sp.dma_start(out[t // NT, (t % NT) * P:(t % NT + 1) * P, :], res[:, t, :])\
                            .then_inc(s["out_done"], 16)
                elif part == "w3" and b == 0:
                    sp.wait_ge(s["st_ps"], 4 * NT * B)
                    sp.dma_start(w3_raw[:], w3.rearrange("(f p) c -> p f c", p=P)).then_inc(s["w3_in"], 16)
            sp.wait_ge(s["out_done"], 16 * B * NT)

        @block.gpsimd
        def _(eng):
            chain = [0]

            def link(ins):
                chain[0] += 1
                ins.then_inc(s["pool_chain"], 1)
                eng.wait_ge(s["pool_chain"], chain[0])

            def split(raw, hi, lo, ok):
                link(eng.tensor_scalar(hi, raw, 1.0, 0.0, ALU.mult, ALU.add))
                eng.tensor_tensor(lo, raw, hi.bitcast(F32), ALU.subtract).then_inc(ok, 1)

            eng.memset(pw[:], -0.5)
            eng.memset(ident_b[:], 0.0)
            eng.memset(causal_b[:], 0.0)
            eng.memset(earlier[:], 1.0)
            link(eng.memset(ident[:], 0.0))
            eng.affine_select(out=ident[:], in_=ident[:], compare_op=ALU.not_equal, fill=1.0, base=0,
                              pattern=[[-1, P]], channel_multiplier=1).then_inc(s["const"], 1)

            def ln_rstd(n, b):
                eng.wait_ge(s[f"ln_mv{n}"], b + 1)
                link(eng.tensor_scalar(vare[:, n, :], mv[:, n, :, 1], EPS, None, ALU.add))
                link(eng.tensor_tensor(rstd[:, n, :], vare[:, n, :], pw[:], ALU.pow))
                link(eng.tensor_tensor(shift[:, n, :], mv[:, n, :, 0], rstd[:, n, :], ALU.mult))
                eng.tensor_scalar(shift[:, n, :], shift[:, n, :], -1.0, None, ALU.mult).then_inc(s[f"ln_rstd{n}"], 1)

            for part, b in steps("POOL"):
                if part == "ln1":
                    ln_rstd(0, b)
                    if b == 0:
                        eng.affine_select(out=ident_b[:], in_=ident_b[:], compare_op=ALU.not_equal, fill=1.0, base=0,
                                          pattern=[[-1, P]], channel_multiplier=1)
                        eng.affine_select(out=earlier[:], in_=earlier[:], compare_op=ALU.is_gt, fill=0.0, base=0,
                                          pattern=[[1, E], [-1, E]], channel_multiplier=0)
                        eng.affine_select(out=causal_b[:], in_=causal_b[:], compare_op=ALU.is_ge, fill=NEG, base=0,
                                          pattern=[[-1, P]], channel_multiplier=1).then_inc(s["const"], 1)
                elif part == "qk":
                    n = b
                    eng.wait_ge(s["rope_ok"], n + 1)
                    if n >= 2:
                        eng.wait_ge(s["stk_hi"], n - 1)
                        eng.wait_ge(s["stk_lo"], n - 1)
                    eng.tensor_tensor(rot[:, n % 2].rearrange("p g (a i) -> p a g i", a=2), rope_c[:], rope_s[:],
                                      ALU.add)\
                        .then_inc(s["rot_ok"], 1)
                elif part == "sh":
                    n = b
                    eng.wait_ge(s["stk_hi"], n + 1)
                    eng.tensor_tensor(stk[:, 0:H, DH:2 * DH], rot[:, n % 2, 0:H, :], stk[:, 0:H, 0:DH].bitcast(F32),
                                      ALU.subtract)
                    eng.tensor_tensor(stk[:, H:2 * H, 2 * DH:3 * DH], rot[:, n % 2, H:2 * H, :],
                                      stk[:, H:2 * H, 0:DH].bitcast(F32), ALU.subtract).then_inc(s["stk_lo"], 1)
                elif part == "tr" and b == 7:
                    eng.wait_ge(s["wo_in"], 16)
                    split(wo_raw[:], wo_hi[:], wo_lo[:], s["wo_ok"])
                    eng.wait_ge(s["gate_in"], 16)
                    split(gate_raw[:], gate_hi[:], gate_lo[:], s["gate_ok"])
                    eng.wait_ge(s["mask_in"], 16)
                    eng.tensor_scalar(mask_add[:], mask_u8[:], -1.0, -NEG, ALU.add, ALU.mult).then_inc(s["mask_ok"], 1)
                elif part == "s":
                    g, i = divmod(b, 3)
                    eng.wait_ge(s["p_exp"], b + 1)
                    v = prob[:, g % 2, i, :].rearrange("p (h q) -> p h q", h=2 if i < 2 else G)[:, :, 0:P]
                    eng.affine_select(out=v, in_=v, compare_op=ALU.is_ge, fill=0.0, base=0,
                                      pattern=[[0, v.shape[1]], [1, P]], channel_multiplier=-1)\
                        .then_inc(s["p_masked"], 1)
                elif part == "h" and b % NG == NG - 1:
                    eng.wait_ge(s["p_hi"], b + 1)
                    eng.tensor_tensor(prob_lo[:, b % 2], prob[:, b % 2], prob_hi[:, b % 2], ALU.subtract)\
                        .then_inc(s["p_lo_last"], 1)
                elif part == "ctx":
                    eng.wait_ge(s["ctx_in"], 16 * (b + 1))
                    split(ctx_raw[:], ctx_hi[:], ctx_lo[:], s["ctx_ok"])
                    eng.wait_ge(s["ctxt_in"], 16 * (b + 1))
                    split(ctxt_raw[:], ctxt_hi[:], ctxt_lo[:], s["ctx_ok"])
                elif part == "w12":
                    raw, hi, lo = up_weights(b)
                    eng.wait_ge(s["w12_hi_ok"], b + 1)
                    eng.tensor_tensor(lo, raw, hi.bitcast(F32), ALU.subtract).then_inc(s["w12_ok"], 1)
                elif part == "w3":
                    j = (b + FE) % FT
                    eng.wait_ge(s["w3_hi_ok"], b + 1)
                    eng.tensor_tensor(w3_lo[:, j], w3_raw[:, j], w3_hi[:, j].bitcast(F32), ALU.subtract)\
                        .then_inc(s["w3_ok"], 1)
                elif part == "ln2":
                    ln_rstd(1, b)
                elif part == "ln3":
                    ln_rstd(2, b)

        @block.scalar
        def _(act):
            def halves_of(ps):
                return ps[:].rearrange("p (k t) -> p k t", k=KC)

            def xn_hi_copy(n, b, dst):
                act.wait_ge(s[f"xnt_ps{n}"], b + 1)
                act.copy(dst, halves_of(ps_x1 if n == 0 else ps_tail)).then_inc(s[f"xn_hi_ok{n}"], 1)

            def normalise(b, n):
                dst = tail if n else xn1
                act.wait_ge(s[f"ln_rstd{n}"], b + 1)
                if n == 0 and b:
                    act.wait_ge(s["xnt_ps0"], b)
                if n:
                    act.wait_ge(s["ot_ps" if n == 1 else "xpt_ps"], b + 1)
                for t in range(NT):
                    ins = act.activation(dst[:, t, :], res[:, NT * b + t, :], ACT.Identity, bias=shift[:, n, t:t + 1],
                                         scale=rstd[:, n, t:t + 1])
                ins.then_inc(s[f"ln_xn{n}"], 1)

            for part, b in steps("ACT"):
                if part in ("ln1n", "ln2n", "ln3n"):
                    normalise(b, int(part[2]) - 1)
                elif part == "w12":
                    if b % UPW == 0:
                        act.wait_ge(s["w1_in" if b == 0 else "w2_in"], 16)
                    raw, hi, lo = up_weights(b)
                    act.copy(hi, raw).then_inc(s["w12_hi_ok"], 1)
                elif part == "w3":
                    if b == 0:
                        act.wait_ge(s["w3_in"], 16)
                    j = (b + FE) % FT
                    act.copy(w3_hi[:, j], w3_raw[:, j]).then_inc(s["w3_hi_ok"], 1)
                elif part == "xt":
                    if b == 0:
                        act.wait_ge(s["w_in"], 16)
                        act.copy(wqkv_hi[:], wqkv_raw[:]).then_inc(s["wqkv_hi_ok"], 1)
                    xn_hi_copy(0, b, xt_hi[:])
                elif part == "v":
                    act.wait_ge(s["v_ps"], b + 1)
                    if b >= 2:
                        act.wait_ge(s["o_ps"], NG * (b - 1))
                    act.copy(v_st[:, b % 2, :, :, 0, 0:DH], ps_x1[:].rearrange("p (t h d) -> p t h d", t=NT, d=DH))\
                        .then_inc(s["v_hi"], 1)
                elif part == "vm":
                    act.wait_ge(s["v_mid"], 2 * b + 1)
                    act.copy(v_st[:, b % 2, :, :, 1, 0:DH], v_r1[:].rearrange("p t (h d) -> p t h d", d=DH))\
                        .then_inc(s["v_hi"], 1)
                elif part == "sh":
                    n = b
                    act.wait_ge(s["rot_ok"], n + 1)
                    if n:
                        act.wait_ge(s["st_ps"], 4 * n)
                    act.copy(stk[:, :, 0:DH], rot[:, n % 2])
                    act.copy(stk[:, 0:H, 2 * DH:3 * DH], rot[:, n % 2, 0:H, :])
                    act.copy(stk[:, H:2 * H, DH:2 * DH], rot[:, n % 2, H:2 * H, :]).then_inc(s["stk_hi"], 1)
                elif part == "tr":
                    n, c = divmod(b, 4)
                    if n // NT >= 2 and n % NT == 0:
                        act.wait_ge(s["s_ps"], 3 * NG * (n // NT - 1))
                    act.wait_ge(s["st_ps"], b + 1)
                    dst = q_t if c < 2 else k_t
                    act.copy(dst[:, n // NT % 2, 4 * (c % 2):4 * (c % 2) + 4, n % NT * P:(n % NT + 1) * P],
                             ps_st[c % 2][:].rearrange("p (j q) -> p j q", j=4)).then_inc(s["st_ok"], 1)
                elif part == "mt":
                    act.wait_ge(s["mt_ps"], b + 1)
                    if b:
                        act.wait_ge(s["shift_ok"], 32 * b)
                    act.copy(negm_t[:], ps_st[0][0:H, 0:S].rearrange("h (t q) -> h t q", t=NT)).then_inc(s["mt_ok"], 1)
                elif part == "s":
                    g, i = divmod(b, 3)
                    act.wait_ge(s["s_ps"], b + 1)
                    if g >= 2:
                        wait_p_lo(act, g - 2)
                    act.activation(prob[:, g % 2, i, :], ps_s[b % 2][:], ACT.Exp, scale=DH ** -0.5)\
                        .then_inc(s["p_exp"], 1)
                elif part == "h":
                    act.wait_ge(s["p_masked"], 3 * b + 3)
                    if b >= 2:
                        act.wait_ge(s["o_ps"], b - 1)
                    act.copy(prob_hi[:, b % 2], prob[:, b % 2]).then_inc(s["p_hi"], 1)
                elif part == "ot":
                    act.wait_ge(s["ot_ps"], b + 1)
                    act.copy(tail_hi[:], halves_of(ps_tail)).then_inc(s["oh_ok"], 1)
                elif part == "t2":
                    xn_hi_copy(1, b, tail_hi[:])
                elif part == "xs":
                    act.wait_ge(s["xs_ok"], b + 1)
                    for t in range(NT):
                        act.activation(tail[:, t, :], tail[:, t, :], ACT.Exp, bias=xs_neg[:, t:t + 1],
                                       accum_out=xs_sum[:, t:t + 1]).then_inc(s["xp_ok"], 1)
                elif part == "pt":
                    act.wait_ge(s["xpt_ps"], b + 1)
                    act.copy(tail_hi[:], halves_of(ps_tail)).then_inc(s["xph_ok"], 1)
                elif part == "t3":
                    xn_hi_copy(2, b, x3_hi[:, :, b * S:(b + 1) * S])
                elif part == "lg":
                    act.wait_ge(s["g_ready"], b + 1)
                    act.activation(g_exp[:], g_sub[:], ACT.Exp).then_inc(s["g_exp_ok"], 1)
                elif part == "ct":
                    act.wait_ge(s["ct_ps"], b + 1)
                    if b:
                        act.wait_ge(s["ct_out"], 16 * b)
                    act.copy(comb_t[:], ps_tail[0:E, 0:S].rearrange("e (t q) -> e t q", t=NT)).then_inc(s["ct_ok"], 1)
                elif part == "up":
                    m = b
                    act.wait_ge(s["h_ps1"], m + 1)
                    if m >= 2:
                        act.wait_ge(s["hg_ok"], m - 1)
                    act.activation(h_s[:, m % 2], h1_bank[m % 2][:], ACT.Silu).then_inc(s["hs_ok"], 1)
                elif part == "dn":
                    m = b
                    act.wait_ge(s["hc_ok"], m + 1)
                    if m >= 2:
                        act.wait_ge(s["w3_done"], m - 1)
                    act.copy(h_hi[:, m % 2], h_c[:, m % 2]).then_inc(s["hhi_ok"], 1)

        @block.vector
        def _(dve):
            chain = [0]

            def link(ins):
                chain[0] += 1
                ins.then_inc(s["dve_chain"], 1)
                dve.wait_ge(s["dve_chain"], chain[0])

            def moments(b, n):
                for t in range(NT):
                    ins = dve.bn_stats(stats[:, n, t, :], res[:, NT * b + t, :])
                link(ins)
                for t in range(NT):
                    ins = dve.bn_aggr(mv[:, n, t, :], stats[:, n, t, :])
                ins.then_inc(s[f"ln_mv{n}"], 1)

            def halves_of(ps):
                return ps[:].rearrange("p (k t) -> p k t", k=KC)

            def xn_lo_sub(n, b, hi, dst):
                dve.wait_ge(s[f"xn_hi_ok{n}"], b + 1)
                dve.tensor_tensor(dst, halves_of(ps_x1 if n == 0 else ps_tail), hi.bitcast(F32), ALU.subtract)\
                    .then_inc(s[f"xn_lo_ok{n}"], 1)

            def maxima(n):
                f = n % 12
                dve.wait_ge(s["sm_ps"], n + 1)
                t, w, j = (0, P, 4 * (f // 2)) if f < 4 else (1, S, 2 * ((f - 4) // 2))
                dve.tensor_reduce(negm[:, t, f % 2, j:j + 512 // w], ps_st[f % 2][:].rearrange("p (j k) -> p j k", k=w),
                                  AX.X, ALU.max, negate=True).then_inc(s["sm_max"], 1)

            dve.memset(stk[:, :, KROWS:SLOT].bitcast(F32), 0.0)
            link(dve.memset(v_st[:, :, :, :, :, DH:VP], 0.0))
            dve.memset(v_st[:, :, :, :, 0, DH:VP], 1.0)
            link(dve.memset(stk[:, H:2 * H, KROWS:KROWS + 1].bitcast(F32), 1.0))

            for part, b in steps("DVE"):
                if part == "ln1":
                    dve.wait_ge(s[f"x_in{b}"], 16)
                    moments(b, 0)
                elif part == "xt":
                    if b == 0:
                        dve.wait_ge(s["wqkv_hi_ok"], 1)
                        dve.tensor_tensor(wqkv_lo[:], wqkv_raw[:], wqkv_hi[:].bitcast(F32), ALU.subtract)\
                            .then_inc(s["wqkv_ok"], 1)
                    xn_lo_sub(0, b, xt_hi[:], xt_lo[:])
                elif part == "v":
                    dve.wait_ge(s["v_hi"], 2 * b + 1)
                    dve.tensor_tensor(v_r1[:].rearrange("p t (h d) -> p t h d", d=DH),
                                      ps_x1[:].rearrange("p (t h d) -> p t h d", t=NT, d=DH),
                                      v_st[:, b % 2, :, :, 0, 0:DH], ALU.subtract).then_inc(s["v_mid"], 1)
                elif part == "vm":
                    dve.wait_ge(s["v_hi"], 2 * b + 2)
                    dve.tensor_tensor(v_st[:, b % 2, :, :, 2, 0:DH], v_r1[:].rearrange("p t (h d) -> p t h d", d=DH),
                                      v_st[:, b % 2, :, :, 1, 0:DH], ALU.subtract).then_inc(s["v_mid"], 1)
                elif part == "qk":
                    t, n = b % NT, b
                    if n == 0:
                        dve.wait_ge(s["tab_in"], 32)
                    dve.wait_ge(s["qk_ps"], n + 1)
                    if n:
                        dve.wait_ge(s["rot_ok"], n)
                    qk = ps_qk[:].rearrange("p (a g i) -> p a g i", a=2, i=DH // 2)
                    dve.tensor_tensor(rope_c[:].rearrange("p a g i -> p (a g) i"), qk.rearrange("p a g i -> p (a g) i"),
                                      cos_t[:, t, None, :].broadcast_to([P, 4 * H, DH // 2]), ALU.mult)
                    for a in range(2):
                        ins = dve.tensor_tensor(rope_s[:, a], qk[:, 1 - a],
                                                sin_t[:, t, a, None, :].broadcast_to([P, 2 * H, DH // 2]), ALU.mult)
                    ins.then_inc(s["rope_ok"], 1)
                elif part == "m":
                    if b and b % 12 == 0:
                        dve.wait_ge(s["mt_ps"], b // 12)
                    maxima(b)
                elif part == "h" and b % NG < NG - 1:
                    dve.wait_ge(s["p_hi"], b + 1)
                    dve.tensor_tensor(prob_lo[:, b % 2], prob[:, b % 2], prob_hi[:, b % 2], ALU.subtract)\
                        .then_inc(s["p_lo"], 1)
                elif part == "pv":
                    g = b % NG
                    dve.wait_ge(s["o_ps"], b + 1)
                    for t in range(NT):
                        heads = o_sum[:, t].rearrange("p (j r) d -> p j r d", r=2)
                        heads = heads[:, G * (g // 2):G * (g // 2) + G, g % 2]
                        parts = ps_out[:, t * G * 3 * VP:(t + 1) * G * 3 * VP]
                        parts = parts.rearrange("p (h a d) -> p h d a", h=G, a=3)
                        dve.tensor_reduce(heads, parts, AX.X, ALU.add).then_inc(s["o_ok"], 1)
                elif part == "on":
                    if b == 0:
                        dve.wait_ge(s["mask_in"], 16)
                        dve.tensor_reduce(valid[:], mask_u8[:], AX.X, ALU.max).then_inc(s["valid_ok"], 1)
                    dve.wait_ge(s["o_ok"], NT * NG * (b + 1))
                    link(dve.reciprocal(o_rec[:], o_sum[:, :, :, DH:VP]))
                    if b:
                        dve.wait_ge(s["xnt_ps2"], b)
                    dve.tensor_tensor(tail[:].rearrange("p t (h d) -> p t h d", h=H), o_sum[:, :, :, 0:DH],
                                      o_rec[:].broadcast_to([P, NT, H, DH]), ALU.mult)\
                        .then_inc(s["on_ok"], 1)
                elif part == "ot":
                    dve.wait_ge(s["oh_ok"], b + 1)
                    dve.tensor_tensor(tail_lo[:], halves_of(ps_tail), tail_hi[:].bitcast(F32), ALU.subtract)\
                        .then_inc(s["ol_ok"], 1)
                elif part == "wo":
                    rb = res[:, NT * b:NT * (b + 1), :]
                    dve.wait_ge(s["wo_ps"], NT * (b + 1))
                    dve.tensor_tensor(rb, ps_tail[:].rearrange("p (t c) -> p t c", t=NT), rb, ALU.add)\
                        .then_inc(s["x1_ok"], 1)
                elif part == "ln2":
                    dve.wait_ge(s["x1_ok"], b + 1)
                    moments(b, 1)
                elif part == "t2":
                    xn_lo_sub(1, b, tail_hi[:], tail_lo[:])
                elif part == "xs":
                    if b == 0:
                        dve.wait_ge(s["mask_ok"], 1)
                    dve.wait_ge(s["xs_ps"], NT * (b + 1))
                    dve.wait_ge(s["xnt_ps1"], b + 1)
                    for t in range(NT):
                        ins = dve.tensor_tensor_reduce(tail[:, t, :], ps_tail[:, t * S:(t + 1) * S], mask_add[:, b, :],
                                                       C ** -0.5, -3e38, ALU.add, ALU.max, xs_max[:, t:t + 1])
                    link(ins)
                    dve.tensor_scalar(xs_neg[:], xs_max[:], -1.0, None, ALU.mult).then_inc(s["xs_ok"], 1)
                elif part == "xc":
                    dve.wait_ge(s["xp_ok"], NT * (b + 1))
                    link(dve.reciprocal(xs_rec[:], xs_sum[:]))
                    dve.wait_ge(s["valid_ok"], 1)
                    link(dve.tensor_scalar(xs_coef[:], xs_rec[:], valid[:, b:b + 1], None, ALU.mult))
                elif part == "pt":
                    dve.wait_ge(s["xph_ok"], b + 1)
                    dve.tensor_tensor(tail_lo[:], halves_of(ps_tail), tail_hi[:].bitcast(F32), ALU.subtract)\
                        .then_inc(s["xpl_ok"], 1)
                elif part == "ro":
                    dve.wait_ge(s["ro_ps"], NT * (b + 1))
                    for t in range(NT):
                        r1 = res[:, NT * b + t, :]
                        dve.scalar_tensor_tensor(out=r1, in0=ps_tail[:, t * C:(t + 1) * C], scalar=xs_coef[:, t:t + 1],
                                                 in1=r1, op0=ALU.mult, op1=ALU.add).then_inc(s["x2_ok"], 1)
                elif part == "ln3":
                    dve.wait_ge(s["x2_ok"], NT * (b + 1))
                    moments(b, 2)
                elif part == "t3":
                    xn_lo_sub(2, b, x3_hi[:, :, b * S:(b + 1) * S], x3_lo[:, :, b * S:(b + 1) * S])
                elif part == "lg":
                    dve.wait_ge(s["lg_ps"], NT * (b + 1))
                    if b == 0:
                        dve.wait_ge(s["const"], 2)
                    lg = ps_tail[:, 0:NT * E].rearrange("p (t e) -> p t e", t=NT)
                    link(dve.tensor_reduce(g_max[:], lg, AX.X, ALU.max))
                    dve.tensor_tensor(g_sub[:], lg, g_max[:, :, None].broadcast_to([P, NT, E]), ALU.subtract)\
                        .then_inc(s["g_ready"], 1)
                elif part == "rk":
                    dve.wait_ge(s["g_exp_ok"], b + 1)
                    link(dve.tensor_reduce(g_sum[:], g_exp[:], AX.X, ALU.add))
                    link(dve.reciprocal(g_rec[:], g_sum[:]))
                    link(dve.tensor_tensor(g_p[:], g_exp[:], g_rec[:, :, None].broadcast_to([P, NT, E]), ALU.mult))
                    for t in range(NT):
                        one = g_p[:, t, :, None].broadcast_to([P, E, E])
                        other = g_p[:, t, None, :].broadcast_to([P, E, E])
                        dve.tensor_tensor(g_gt[:, t], other, one, ALU.is_gt)
                        ins = dve.tensor_tensor(g_eq[:, t], other, one, ALU.is_equal)
                    link(ins)
                    for t in range(NT):
                        ins = dve.tensor_tensor(g_eq[:, t], g_eq[:, t], earlier[:], ALU.mult)
                    link(ins)
                    link(dve.tensor_tensor(g_gt[:], g_gt[:], g_eq[:], ALU.add))
                    link(dve.tensor_reduce(g_rank[:], g_gt[:], AX.X, ALU.add))
                    dve.scalar_tensor_tensor(out=comb[:], in0=g_rank[:], scalar=2.0, in1=g_p[:], op0=ALU.is_lt,
                                             op1=ALU.mult).then_inc(s["comb_ok"], 1)
                elif part == "up":
                    m = b
                    g, n = divmod(m, FT)
                    j = (n + FE) % FT
                    dve.wait_ge(s["hs_ok"], m + 1)
                    dve.wait_ge(s["h_ps2"], m + 1)
                    if m >= 2:
                        dve.wait_ge(s["hlo_ok"], m - 1)
                        dve.wait_ge(s["hhi_ok"], m - 1)
                    ins = dve.tensor_tensor(h_c[:, m % 2], h2_bank[m % 2][:], h_s[:, m % 2], ALU.mult)
                    if j >= FE:
                        ins.then_inc(s["hg_ok"], 1)
                        dve.wait_ge(s["hg_ok"], m + 1)
                        dve.sem_inc(s["hc_ok"], 1)
                    else:
                        ins.then_inc(s["hg_ok"], 1)
                        dve.wait_ge(s["cb_in"], 16 * CB * (g + 1))
                        dve.wait_ge(s["hg_ok"], m + 1)
                        dve.tensor_tensor(h_c[:, m % 2], h_c[:, m % 2], comb_b[:, j, :], ALU.mult)\
                            .then_inc(s["hc_ok"], 1)
                elif part == "dn":
                    m = b
                    dve.wait_ge(s["hhi_ok"], m + 1)
                    dve.tensor_tensor(h_lo[:, m % 2], h_c[:, m % 2], h_hi[:, m % 2].bitcast(F32), ALU.subtract)\
                        .then_inc(s["hlo_ok"], 1)
                elif part == "y":
                    for t in range(4):
                        if t < 2:
                            dve.wait_ge(s["y_ps"], b + 1)
                        else:
                            dve.wait_ge(s["w3_done"], FT * (b + 1))
                        dve.tensor_tensor(res[:, 4 * b + t, :], y_tile(t), res[:, 4 * b + t, :], ALU.add)\
                            .then_inc(s["y_ok"], 1)

        @block.tensor
        def _(pe):
            def split_product(dst, lhs_hi, lhs_lo, rhs_hi, rhs_lo, kt=KC):
                for k in range(kt):
                    for i, (a, c) in enumerate(halves(lhs_hi, lhs_lo, rhs_hi, rhs_lo)):
                        ins = pe.matmul(dst, a(k), c(k), start=(k == 0 and i == 0), stop=(k == kt - 1 and i == 2))
                return ins

            def transposes(dst, src):
                for k in range(2):
                    for t in range(NT):
                        ins = pe.transpose(dst[:, k * S + t * P:k * S + (t + 1) * P], src(t, k), ident[:])
                return ins

            def head_rows(tensor, b, h, rows):
                r = SLOT * (h % 2)
                return tensor[r:r + rows, b % 2, h // 2, :]

            def product(dst0, dst1, a_hi, a_lo, w_hi, w_lo, name):
                for t, dst in enumerate((dst0, dst1)):
                    tok = slice(t * P, (t + 1) * P)
                    split_product(dst, lambda k: a_hi[:, k, tok], lambda k: a_lo[:, k, tok],
                                  lambda k: w_hi[:, k, :], lambda k: w_lo[:, k, :]).then_inc(s[name], 1)

            def row_maxima_scores(b, f):
                if f >= 2:
                    pe.wait_ge(s["sm_max"], 12 * b + f - 1)
                t = 0 if f < 4 else 1
                keys = P * (t + 1)
                for i in range(512 // keys):
                    h = 2 * (4 * (f // 2) + i if t == 0 else 2 * ((f - 4) // 2) + i) + f % 2
                    dst = ps_st[f % 2][:, i * keys:(i + 1) * keys]
                    pe.matmul(dst, head_rows(q_t, b, h, KROWS)[:, t * P:(t + 1) * P],
                              head_rows(k_t, b, h, KROWS)[:, 0:keys], start=True, stop=True)
                    ins = pe.matmul(dst[:, t * P:keys], ident_b[:], causal_b[:], start=False, stop=True,
                                    skip_group_check=True)
                ins.then_inc(s["sm_ps"], 1)

            def scores(b, g, i):
                n = 3 * (NG * b + g) + i
                if n >= 2:
                    pe.wait_ge(s["p_exp"], n - 1)
                k0 = 0 if i < 2 else P
                for c in range(2 if i < 2 else G):
                    h = head(g, 2 * i + c if i < 2 else c)
                    ins = pe.matmul(ps_s[n % 2][:, c * (S - k0):(c + 1) * (S - k0)],
                                    head_rows(k_t, b, h, KROWS + 1)[:, k0:k0 + P],
                                    head_rows(q_t, b, h, KROWS + 1)[:, k0:S], start=True, stop=True)
                ins.then_inc(s["s_ps"], 1)

            def values(b, g):
                n = NG * b + g
                pe.wait_ge(s["p_hi"], n + 1)
                wait_p_lo(pe, n)
                if g == 0:
                    pe.wait_ge(s["v_mid"], 2 * (b + 1))
                if n:
                    pe.wait_ge(s["o_ok"], NT * n)
                for t in range(NT):
                    for i in range(G):
                        o = (t * G + i) * 3 * VP
                        parts = [(pr, 0, i // 2, (i % 2) * S + t * P) for pr in (prob_hi, prob_lo)]
                        if t:
                            parts += [(pr, 1, 2, i * P) for pr in (prob_hi, prob_lo)]
                        for m, (pr, kt, blk, q0) in enumerate(parts):
                            ins = pe.matmul(ps_out[:, o:o + 3 * VP], pr[:, g % 2, blk, q0:q0 + P],
                                            v_st[:, b % 2, kt, head(g, i)].rearrange("p a d -> p (a d)"),
                                            start=(m == 0), stop=(m == len(parts) - 1))
                ins.then_inc(s["o_ps"], 1)

            def up(m):
                g, n = divmod(m, FT)
                j = (n + FE) % FT
                if m >= 2:
                    pe.wait_ge(s["hg_ok"], m - 1)
                hid = slice(j * P, (j + 1) * P)
                tok = slice(g * GT, (g + 1) * GT)
                for w_hi, w_lo, bk, name in ((w1_hi, w1_lo, h1_bank, "h_ps1"), (w2_hi, w2_lo, h2_bank, "h_ps2")):
                    split_product(bk[m % 2][:], lambda k: w_hi[:, k, hid], lambda k: w_lo[:, k, hid],
                                  lambda k: x3_hi[:, k, tok], lambda k: x3_lo[:, k, tok]).then_inc(s[name], 1)

            def down(m):
                g, n = divmod(m, FT)
                j = (n + FE) % FT
                pe.wait_ge(s["hlo_ok"], m + 1)
                pe.wait_ge(s["hhi_ok"], m + 1)
                if not g:
                    pe.wait_ge(s["w3_ok"], n + 1)
                for t in range(4):
                    if g and n == 0:
                        pe.wait_ge(s["y_ok"], 2 * (t // 2) + 2)
                    tok = slice(t * P, (t + 1) * P)
                    for i, (a, c) in enumerate(halves(h_hi, h_lo, w3_hi, w3_lo)):
                        ins = pe.matmul(y_tile(t), a[:, m % 2, tok], c[:, j, :],
                                        start=(n == 0 and i == 0 and t % 2 == 0), stop=(n == FT - 1 and i == 2),
                                        skip_group_check=True)
                    if n == FT - 1 and t == 1:
                        ins.then_inc(s["y_ps"], 1)
                ins.then_inc(s["w3_done"], 1)

            out_tiles = [ps_tail[:, t * C:(t + 1) * C] for t in range(NT)]
            pe.wait_ge(s["const"], 1)
            for part, b in steps("PE"):
                if part == "xt":
                    pe.wait_ge(s["ln_xn0"], b + 1)
                    if b:
                        pe.wait_ge(s["v_mid"], 2 * b - 1)
                    transposes(ps_x1, lambda t, k: xn1[:, t, k * P:(k + 1) * P]).then_inc(s["xnt_ps0"], 1)
                elif part == "v":
                    pe.wait_ge(s["xn_lo_ok0"], b + 1)
                    pe.wait_ge(s["wqkv_ok"], 1)
                    for t in range(NT):
                        tok = slice(t * P, (t + 1) * P)
                        ins = split_product(ps_x1[:, t * C:(t + 1) * C], lambda k: xt_hi[:, k, tok],
                                            lambda k: xt_lo[:, k, tok], lambda k: wqkv_hi[:, k, 2 * C:3 * C],
                                            lambda k: wqkv_lo[:, k, 2 * C:3 * C])
                    ins.then_inc(s["v_ps"], 1)
                elif part == "qk":
                    tok = slice(b % NT * P, (b % NT + 1) * P)
                    if b:
                        pe.wait_ge(s["rope_ok"], b)
                    split_product(ps_qk[:], lambda k: xt_hi[:, k, tok], lambda k: xt_lo[:, k, tok],
                                  lambda k: wqkv_hi[:, k, 0:2 * C], lambda k: wqkv_lo[:, k, 0:2 * C])\
                        .then_inc(s["qk_ps"], 1)
                elif part == "tr":
                    n, c = divmod(b, 4)
                    if c == 0:
                        pe.wait_ge(s["stk_lo"], n + 1)
                        if n and n % NT == 0:
                            pe.wait_ge(s["mt_ok"], n // NT)
                            pe.wait_ge(s["sm_max"], 12 * (n // NT))
                    if b >= 2:
                        pe.wait_ge(s["st_ok"], b - 1)
                    for j in range(4):
                        h = 8 * c + 2 * j
                        ins = pe.transpose(ps_st[c % 2][:, j * P:(j + 1) * P],
                                           stk[:, h:h + 2, :].bitcast(F32).rearrange("p h r -> p (h r)"), ident[:])
                    ins.then_inc(s["st_ps"], 1)
                elif part == "m":
                    if b % 12 == 0:
                        pe.wait_ge(s["st_ok"], 4 * NT * (b // 12 + 1))
                        if b == 0:
                            pe.wait_ge(s["const"], 2)
                    row_maxima_scores(*divmod(b, 12))
                elif part == "mt":
                    pe.wait_ge(s["sm_max"], 12 * (b + 1))
                    for t in range(NT):
                        ins = pe.transpose(ps_st[0][0:H, t * P:(t + 1) * P],
                                           negm[:, t].rearrange("p r j -> p (r j)"), ident[:])
                    ins.then_inc(s["mt_ps"], 1)
                elif part == "s":
                    if b % 12 == 0:
                        pe.wait_ge(s["shift_ok"], 32 * (b // 12 + 1))
                    scores(b // 12, b // 3 % NG, b % 3)
                elif part == "pv":
                    values(*divmod(b, NG))
                elif part in ("ot", "t2", "pt", "t3"):
                    ready, n, done = {"ot": ("on_ok", 1, "ot_ps"), "t2": ("ln_xn1", 1, "xnt_ps1"),
                                      "pt": ("xp_ok", NT, "xpt_ps"), "t3": ("ln_xn2", 1, "xnt_ps2")}[part]
                    pe.wait_ge(s[ready], n * (b + 1))
                    if b and part == "ot":
                        pe.wait_ge(s["ct_ok"], b)
                    transposes(ps_tail, lambda t, k: tail[:, t, k * P:(k + 1) * P]).then_inc(s[done], 1)
                elif part == "wo":
                    pe.wait_ge(s["ol_ok"], b + 1)
                    pe.wait_ge(s["wo_ok"], 1)
                    product(*out_tiles, tail_hi, tail_lo, wo_hi, wo_lo, "wo_ps")
                elif part == "xs":
                    pe.wait_ge(s["xn_lo_ok1"], b + 1)
                    pe.wait_ge(s["ctx_ok"], 2 * (b + 1))
                    product(*out_tiles, tail_hi, tail_lo, ctxt_hi, ctxt_lo, "xs_ps")
                elif part == "ro":
                    pe.wait_ge(s["xpl_ok"], b + 1)
                    product(*out_tiles, tail_hi, tail_lo, ctx_hi, ctx_lo, "ro_ps")
                elif part == "lg":
                    pe.wait_ge(s["xn_lo_ok2"], b + 1)
                    pe.wait_ge(s["gate_ok"], 1)
                    for t in range(NT):
                        tok = slice((NT * b + t) * P, (NT * b + t + 1) * P)
                        split_product(ps_tail[:, t * E:(t + 1) * E], lambda k: x3_hi[:, k, tok],
                                      lambda k: x3_lo[:, k, tok], lambda k: gate_hi[:, k, :],
                                      lambda k: gate_lo[:, k, :]).then_inc(s["lg_ps"], 1)
                elif part == "ct":
                    pe.wait_ge(s["comb_ok"], b + 1)
                    for t in range(NT):
                        ins = pe.transpose(ps_tail[0:E, t * P:(t + 1) * P], comb[:, t, :], ident[:])
                    ins.then_inc(s["ct_ps"], 1)
                elif part == "up":
                    m = b
                    g, n = divmod(m, FT)
                    if m == 0:
                        pe.wait_ge(s["w12_ok"], 2 * UPW)
                        pe.wait_ge(s["mt_ok"], B)
                        pe.wait_ge(s["p_exp"], 3 * NG * B)
                        pe.wait_ge(s["xn_lo_ok2"], GT // S)
                    if m == FT:
                        pe.wait_ge(s["xn_lo_ok2"], B)
                    up(m)
                elif part == "dn":
                    down(b)


def kernel(**inputs):
    import numpy as np
    import concourse.bacc as bacc
    from concourse.bass_utils import run_bass_kernel_spmd

    a = {k: np.asarray(v) for k, v in inputs.items()}
    order = np.arange(C).reshape(H, DH // 2, 2).transpose(2, 0, 1).reshape(2, -1)
    columns = np.concatenate([order[0], C + order[0], order[1], C + order[1], 2 * C + np.arange(C)])
    hidden = FT * P

    def up(w, shared):
        return np.concatenate([w.reshape(E * I, C), shared, np.zeros((hidden - E * I - IS, C), w.dtype)]).T

    w3 = a["L0_ffn_w3"]
    down = np.concatenate([w3.transpose(0, 2, 1).reshape(E * I, C), a["L0_ffn_sw3"].T,
                           np.zeros((hidden - E * I - IS, C), w3.dtype)])
    inv = (1.0 / np.float32(10000.0) ** (2.0 * np.arange(DH // 2, dtype=np.float32) / DH)).astype(np.float32)
    angle = np.outer(np.arange(S, dtype=np.float32), inv).astype(np.float32)
    arrays = {
        "x": a["x"], "ctx": a["ctx_2048"], "ctx_t": a["ctx_2048"].transpose(0, 2, 1), "mask": a["mask_BxS2_bk0"],
        "wqkv": a["L0_attn_Wqkv"][:, columns], "wo": a["L0_attn_Wo"], "gate": a["L0_ffn_gate_w"].T,
        "w1": up(a["L0_ffn_w1"], a["L0_ffn_sw1"]), "w2": up(a["L0_ffn_w2"], a["L0_ffn_sw2"]), "w3": down,
        "cos": np.cos(angle), "sin": np.stack([-np.sin(angle), np.sin(angle)], axis=1),
    }
    arrays = {k: np.ascontiguousarray(v) for k, v in arrays.items()}
    nc = bacc.Bacc("TRN2", target_bir_lowering=False, num_devices=1)
    args = [nc.dram_tensor(k, v.shape, mybir.dt.from_np(v.dtype), kind="ExternalInput").ap() for k, v in arrays.items()]
    out = nc.dram_tensor("out", (B, S, C), F32, kind="ExternalOutput").ap()
    decoder_layer(nc, *args, out)
    r = run_bass_kernel_spmd(nc, [arrays], core_ids=[0])
    return r.results[0]["out"]
```
